# Optimizing a Trainium2 kernel written in Bass

```python
import numpy as np
import jax
import jax.numpy as jnp

def _softmax(x, axis=-1):
    return jax.nn.softmax(x, axis=axis)

def _gelu(x):
    return jax.nn.gelu(x, approximate=True)

def _silu(x):
    return jax.nn.silu(x)

def _sigmoid(x):
    return jax.nn.sigmoid(x)

def _layernorm(x, axis=-1, eps=1e-05):
    m = jnp.mean(x, axis=axis, keepdims=True)
    v = jnp.var(x, axis=axis, keepdims=True)
    return (x - m) / jnp.sqrt(v + eps)

def _scatter_add(tgt, idx, src, axis=0):
    return tgt.at[idx].add(src)

def _segment_sum(src, seg, n):
    return jax.ops.segment_sum(src, seg, n)
kernel_name = 'mk_adj_resnorm_d2_adj_r2_8bdda2'

def setup_inputs(seed: int=0):
    np.random.seed(seed)
    _w = jnp.asarray

    def _rec_inputs():
        import jax
        import jax.numpy as jnp
        _gk = jax.random.key(seed)
        x = -0.000929 + 1 * jax.random.normal(jax.random.fold_in(_gk, 1), (8192, 128), jnp.float32)
        _a = jax.random.bernoulli(jax.random.fold_in(_gk, 2), 0.00195312, (8192, 8192))
        _a = jnp.logical_or(_a, jnp.swapaxes(_a, -1, -2))
        _a = jnp.logical_or(_a, jnp.eye(8192, dtype=bool))
        _af = _a.astype(jnp.float32)
        _af = _af * jax.random.uniform(jax.random.fold_in(_gk, 3), (8192, 8192), jnp.float32, 0.05, 1)
        adj = _af
        return (x, adj)
    x, adj = _rec_inputs()

    def _L0_gnn_setup():
        import jax, jax.numpy as jnp
        import numpy as np
        import math
        N = 4096
        D_IN = 128
        H = 128
        GATE_TEMPERATURE = 1.0
        LN_EPS = 1e-05
        key = jax.random.key(seed)
        ks = jax.random.split(key, 10)
        s_msg = 1.0 / math.sqrt(D_IN)
        s_gate = 1.0 / math.sqrt(H)
        s_upd = 1.0 / math.sqrt(D_IN + H)
        return {'node_features': jax.random.normal(ks[0], (N, D_IN), dtype=jnp.float32), 'adj_matrix': jax.random.uniform(ks[1], (N, N), dtype=jnp.float32), 'recency_prior': jax.random.uniform(ks[2], (N, N), dtype=jnp.float32), 'W_msg': jax.random.uniform(ks[3], (D_IN, H), jnp.float32, -s_msg, s_msg), 'b_msg': jax.random.uniform(ks[4], (H,), jnp.float32, -s_msg, s_msg), 'W_q': jax.random.uniform(ks[5], (H, H), jnp.float32, -s_gate, s_gate), 'W_k': jax.random.uniform(ks[6], (H, H), jnp.float32, -s_gate, s_gate), 'gate_bias': jnp.float32(-1.0), 'W_upd': jax.random.uniform(ks[7], (D_IN + H, H), jnp.float32, -s_upd, s_upd), 'b_upd': jax.random.uniform(ks[8], (H,), jnp.float32, -s_upd, s_upd), 'ln_gamma': jnp.ones((H,), jnp.float32), 'ln_beta': jnp.zeros((H,), jnp.float32)}
    _L0_gnn_all = _L0_gnn_setup()
    _L0_gnn_in = {k: v for k, v in _L0_gnn_all.items() if k in ('W_msg', 'b_msg', 'W_q', 'W_k', 'gate_bias', 'W_upd', 'b_upd', 'ln_gamma', 'ln_beta')}
    del _L0_gnn_all

    def _L1_gnn_setup():
        import jax, jax.numpy as jnp
        import numpy as np
        N = 4096
        F = 128
        U = 128
        EDGE_P = 0.002

        def adj_norm(adj):
            a_hat = adj + jnp.eye(adj.shape[0], dtype=adj.dtype)
            d_inv_sqrt = jax.lax.rsqrt(jnp.sum(a_hat, axis=-1))
            return a_hat * d_inv_sqrt[:, None] * d_inv_sqrt[None, :]
        key = jax.random.key(seed)
        k1, k2, k3 = jax.random.split(key, 3)
        a = (jax.random.uniform(k1, (N, N)) < EDGE_P).astype(jnp.float32)
        adj = jnp.maximum(a, a.T)
        x = jax.random.normal(k2, (N, F), dtype=jnp.float32)
        W = jax.random.normal(k3, (F, U), dtype=jnp.float32) * 0.05
        b = jnp.zeros((U,), dtype=jnp.float32)
        return {'x': x, 'adj': adj, 'W': W, 'b': b}
    _L1_gnn_all = _L1_gnn_setup()
    _L1_gnn_in = {k: v for k, v in _L1_gnn_all.items() if k in ('W', 'b')}
    del _L1_gnn_all
    return {'x': x, 'adj': adj, 'L0_gnn_W_msg': _L0_gnn_in['W_msg'], 'L0_gnn_b_msg': _L0_gnn_in['b_msg'], 'L0_gnn_W_q': _L0_gnn_in['W_q'], 'L0_gnn_W_k': _L0_gnn_in['W_k'], 'L0_gnn_gate_bias': _L0_gnn_in['gate_bias'], 'L0_gnn_W_upd': _L0_gnn_in['W_upd'], 'L0_gnn_b_upd': _L0_gnn_in['b_upd'], 'L0_gnn_ln_gamma': _L0_gnn_in['ln_gamma'], 'L0_gnn_ln_beta': _L0_gnn_in['ln_beta'], 'L1_gnn_W': _L1_gnn_in['W'], 'L1_gnn_b': _L1_gnn_in['b']}

def reference(x, adj, L0_gnn_W_msg, L0_gnn_b_msg, L0_gnn_W_q, L0_gnn_W_k, L0_gnn_gate_bias, L0_gnn_W_upd, L0_gnn_b_upd, L0_gnn_ln_gamma, L0_gnn_ln_beta, L1_gnn_W, L1_gnn_b):
    import jax
    import jax.numpy as jnp

    def _L0_gnn_ref(node_features, adj_matrix, recency_prior, W_msg, b_msg, W_q, W_k, gate_bias, W_upd, b_upd, ln_gamma, ln_beta):
        import jax, jax.numpy as jnp
        import numpy as np
        import math
        N = 4096
        D_IN = 128
        H = 128
        GATE_TEMPERATURE = 1.0
        LN_EPS = 1e-05
        messages = node_features @ W_msg + b_msg
        q = messages @ W_q
        k = messages @ W_k
        scale = math.sqrt(H) * max(GATE_TEMPERATURE, 1e-06)
        logits = q @ k.T / scale + gate_bias
        probs = jax.nn.sigmoid(logits)
        gates_masked = probs * adj_matrix * recency_prior
        aggregated = gates_masked @ messages
        updated = jnp.concatenate([node_features, aggregated], axis=1) @ W_upd + b_upd
        updated = jax.nn.relu(updated)
        mu = jnp.mean(updated, axis=-1, keepdims=True)
        var = jnp.var(updated, axis=-1, keepdims=True)
        out = (updated - mu) * jax.lax.rsqrt(var + LN_EPS) * ln_gamma + ln_beta
        return out

    def _L1_gnn_ref(x, adj, W, b):
        import jax, jax.numpy as jnp
        import numpy as np
        N = 4096
        F = 128
        U = 128
        EDGE_P = 0.002

        def adj_norm(adj):
            a_hat = adj + jnp.eye(adj.shape[0], dtype=adj.dtype)
            d_inv_sqrt = jax.lax.rsqrt(jnp.sum(a_hat, axis=-1))
            return a_hat * d_inv_sqrt[:, None] * d_inv_sqrt[None, :]
        adj_n = adj_norm(adj)
        h = adj_n @ x
        h = h @ W + b
        return jax.nn.relu(h)
    x = _layernorm(x + _L0_gnn_ref(x, adj, adj, L0_gnn_W_msg, L0_gnn_b_msg, L0_gnn_W_q, L0_gnn_W_k, L0_gnn_gate_bias, L0_gnn_W_upd, L0_gnn_b_upd, L0_gnn_ln_gamma, L0_gnn_ln_beta), axis=-1)
    x = _layernorm(x + _L1_gnn_ref(x, adj, L1_gnn_W, L1_gnn_b), axis=-1)
    return x

_drawn_inputs = setup_inputs


def setup_inputs(seed=0):
    import zlib

    import numpy as np

    out = dict(_drawn_inputs(seed))
    spreads = {'L0_gnn_ln_gamma': (1.0, 0.2), 'L0_gnn_ln_beta': (0.0, 0.1), 'L1_gnn_b': (0.0, 0.1)}
    factors = {}
    for name, (base, spread) in spreads.items():
        noise = np.random.default_rng([zlib.crc32(name.encode()), seed]).standard_normal(out[name].shape)
        drawn = base * np.exp(spread * noise) if base else spread * noise
        out[name] = jnp.asarray(drawn.astype(out[name].dtype))
    for name, factor in factors.items():
        out[name] = (out[name] * factor).astype(out[name].dtype)
    return out
```

```python
import concourse.bass as bass
from concourse import mybir
from contextlib import ExitStack

F32 = mybir.dt.float32
F32R = mybir.dt.float32r
BF16 = mybir.dt.bfloat16
ALU = mybir.AluOpType
ACT = mybir.ActivationFunctionType

N, D = 8192, 128
P = 128
BLK = 32
CH = 1024
RANGE = 2048
NJ = N // CH
NI = N // RANGE
A = P // BLK
KT = CH // P
C = CH // BLK
BANK = 512
HALVES = RANGE // CH
PAIR = 2
BODIES = NJ // PAIR
CHUNKS = PAIR * HALVES
UNITS = CHUNKS * KT
NAT = 2
ATB = 2
EPS = 1e-5
DMA = 16


def build(nc, x, adj, W_msg, b_msg, W_q, W_k, gate_bias, W_upd, b_upd, ln_gamma, ln_beta, W1, b1, out):
    q_dram = nc.dram_tensor("q_split", (P, 2, N), F32, kind="Internal").ap()
    k_dram = nc.dram_tensor("k_split", (P, 2, N), F32, kind="Internal").ap()
    m_dram = nc.dram_tensor("messages", (NJ, P, CH), F32, kind="Internal").ap()
    xT_dram = nc.dram_tensor("x_transposed", (P, N), F32, kind="Internal").ap()
    x1_dram = nc.dram_tensor("x_layer1", (NJ, P, CH), F32, kind="Internal").ap()

    ctx = ExitStack()
    with ctx:
        def sb(name, shape, dt=F32):
            return ctx.enter_context(nc.sbuf_tensor(name, shape, dt))

        def sem(name):
            return ctx.enter_context(nc.semaphore(name))

        nat = [sb(f"nat{n}", [P, C, A * BLK * KT // A]) for n in range(NAT)]
        adjT = [sb(f"adjT{n}", [P, CH]) for n in range(ATB)]
        q_sb = sb("q_sb", [P, 2, RANGE], F32R)
        k_sb = [sb(f"k_sb{n}", [P, 2, CH], F32R) for n in range(PAIR)]
        work = sb("work", [P, 4, 2 * CH])
        sq = [work[:, 0, n * CH:(n + 1) * CH] for n in range(2)]
        gated = [work[:, 1, n * CH:(n + 1) * CH] for n in range(2)]
        m_sb = [work[:, 2, n * CH:(n + 1) * CH] for n in range(PAIR)]
        degp = work[:, 3, :]
        y_all = work[:, :, :].rearrange("p a b -> p (a b)")
        y_sb = [sb(f"y_sb{n}", [P, CH]) for n in range(PAIR)]
        cols = sb("cols", [P, N])
        sT = sb("sT", [P, RANGE])
        stage_a = sb("stage_a", [P, CH])
        stage_b = sb("stage_b", [P, CH])
        stage_c = sb("stage_c", [P, CH])
        stage_d = sb("stage_d", [P, CH])
        ident = sb("ident", [P, P])
        zeros = sb("zeros", [P, BANK], BF16)
        ones = sb("ones", [P, 1])
        ones_row = sb("ones_row", [1, P])
        w_ut, w_ub, w_1 = (sb(n, [P, D]) for n in ("w_ut", "w_ub", "w_1"))
        w_msg, w_q, w_k = (sT[:, n * D:(n + 1) * D] for n in range(3))
        vec_rows = sT[0:1, CH:CH + 3 * D]
        bm_col, bu_col, gb_col, eps_col, one_col = (sb(n, [P, 1]) for n in
                                                    ("bm_col", "bu_col", "gb_col", "eps_col", "one_col"))
        vec_all = sb("vec_all", [P, 3, D])
        deg = sb("deg", [P, NJ * KT])
        root = sb("root", [P, NJ * KT])
        dinv = sb("dinv", [P, NJ * KT])
        stats = sb("stats", [P, KT, 6])
        mv = sb("mv", [P, KT, 2])
        sd = sb("sd", [P, KT])
        rstd = sb("rstd", [P, KT])

        acc = ctx.enter_context(nc.psum_tensor("acc", [P, RANGE], F32))
        lg = [ctx.enter_context(nc.psum_tensor(f"lg{n}", [P, CH], F32)) for n in range(2)]

        def sems(*names):
            return [sem(n) for n in names]

        const_loaded, made, vec_ps, vec_done = sems("const_loaded", "made", "vec_ps", "vec_done")
        x_in, xT_ps, xT_ready, mT_ps, mT_ready, qk_ps, qk_hi, qk_lo, m_ps, m_ready = sems(
            "x_in", "xT_ps", "xT_ready", "mT_ps", "mT_ready", "qk_ps", "qk_hi", "qk_lo", "m_ps", "m_ready")
        stored_x, stored_qk, stored_m = sems("stored_x", "stored_qk", "stored_m")
        nat_in = [sems(f"nat_in{n}_sp", f"nat_in{n}_act") for n in range(NAT)]
        adjT_ready = sem("adjT_ready")
        sq_ready, logits_ready, probs_ready, gated_ready, agg_done, deg_added = sems(
            "sq_ready", "logits_ready", "probs_ready", "gated_ready", "agg_done", "deg_added")
        q_in = sems(*[f"q_in{h}" for h in range(HALVES)])
        stat_in = sems(*[f"stat_in{n}" for n in range(PAIR)])
        range_done, acc_read, deg_ps, deg_read, deg_clear = sems(
            "range_done", "acc_read", "deg_ps", "deg_read", "deg_clear")
        root_ready, dinv_ready, xs_in, upd_ps, upd_ready, rows_ps, x1_rows, x1_out, y_rows, yT_ps, yT_ready, \
            y_kept = sems("root_ready", "dinv_ready", "xs_in", "upd_ps", "upd_ready", "rows_ps", "x1_rows",
                          "x1_out", "y_rows", "yT_ps", "yT_ready", "y_kept")
        var_ready, sd_ready, step = sems("var_ready", "sd_ready", "step")
        y_staged, hop_done, hop_range, s_ready, z_ps, x1_in, rows_done, out_done = sems(
            "y_staged", "hop_done", "hop_range", "s_ready", "z_ps", "x1_in", "rows_done", "out_done")

        block = ctx.enter_context(nc.Block())

        TURNS = NI * BODIES
        ALL = TURNS * UNITS

        def permuted(t):
            return t.rearrange("p (a k r) -> p k a r", a=A, k=KT)

        def stored(t):
            return t.rearrange("p (k a r) -> p k a r", a=A, k=KT)

        def by_slot(t):
            return t.rearrange("p (k d) -> p k d", k=KT)

        def load_chunk(eng, who, turn, ch):
            i0 = (turn // BODIES) * RANGE + (ch % HALVES) * CH
            j0 = (turn % BODIES) * (PAIR * CH) + (ch // HALVES) * CH
            for a in (2 * who, 2 * who + 1):
                src = adj[bass.ds(i0, CH), bass.ds(j0 + a * (CH // A), CH // A)]
                eng.dma_start(nat[ch % NAT][a * BLK:(a + 1) * BLK, :, :],
                              src.rearrange("(c s) w -> s c w", s=BLK)).then_inc(nat_in[ch % NAT][who], DMA)

        def next_chunk(eng, who, turn, ch):
            if ch + NAT < CHUNKS:
                load_chunk(eng, who, turn, ch + NAT)
            else:
                load_chunk(eng, who, (turn + 1) % TURNS, ch + NAT - CHUNKS)

        def unit(u):
            ch = u // KT
            return ch, ch // HALVES, ch % HALVES, u % KT

        def banks(half):
            return [slice(half * CH + b * BANK, half * CH + (b + 1) * BANK) for b in range(CH // BANK)]

        @block.sync
        def _(sp):
            for dst, src in ((w_msg, W_msg), (w_q, W_q), (w_k, W_k), (w_1, W1),
                             (w_ut, W_upd[0:D, :]), (w_ub, W_upd[D:2 * D, :])):
                sp.dma_start(dst[:, :], src).then_inc(const_loaded, DMA)
            for dst, src in ((bm_col, b_msg), (bu_col, b_upd)):
                sp.dma_start(dst[:, :], src.rearrange("(d o) -> d o", o=1)).then_inc(const_loaded, DMA)
            sp.dma_start(gb_col[:, :], gate_bias.rearrange("(a b) -> a b", b=1).to_broadcast([P, 1])
                         ).then_inc(const_loaded, DMA)
            for n, src in enumerate((ln_gamma, ln_beta, b1)):
                sp.dma_start(vec_rows[:, n * D:(n + 1) * D], src.rearrange("(a d) -> a d", a=1)
                             ).then_inc(const_loaded, DMA)

            def load_x(g):
                sp.dma_start(by_slot(stage_a[:, :]),
                             x[bass.ds(g * CH, CH), :].rearrange("(k p) d -> p k d", p=P)).then_inc(x_in, DMA)

            load_x(0)
            for ch in range(NAT):
                load_chunk(sp, 0, 0, ch)
            with sp.Fori(0, NJ) as g:
                sp.wait_ge(xT_ready, g + 1)
                sp.dma_start(xT_dram[:, bass.ds(g * CH, CH)], stage_b[:, :]).then_inc(stored_x, DMA)
                load_x((g + 1) % NJ)
                sp.wait_ge(qk_lo, 2 * g + 2)
                sp.dma_start(q_dram[:, :, bass.ds(g * CH, CH)], q_sb[:, :, 0:CH].bitcast(F32)).then_inc(stored_qk, DMA)
                sp.dma_start(k_dram[:, :, bass.ds(g * CH, CH)], k_sb[0][:, :, :].bitcast(F32)).then_inc(stored_qk, DMA)
                sp.wait_ge(m_ready, g + 1)
                sp.dma_start(m_dram[bass.ds(g, 1), :, :].rearrange("g p w -> (g p) w"), stage_d[:, :]
                             ).then_inc(stored_m, DMA)
            sp.wait_ge(x_in, (NJ + 1) * DMA)
            sp.wait_ge(stored_x, NJ * DMA)
            sp.wait_ge(stored_qk, 2 * NJ * DMA)
            sp.wait_ge(stored_m, NJ * DMA)

            def load_q(half, rg):
                sp.dma_start(q_sb[:, :, half * CH:(half + 1) * CH].bitcast(F32),
                             q_dram[:, :, bass.ds(rg * RANGE + half * CH, CH)]).then_inc(q_in[half], DMA)

            def load_stationary(n, turn):
                jc = (turn % BODIES) * PAIR + n
                sp.dma_start(k_sb[n][:, :, :].bitcast(F32), k_dram[:, :, bass.ds(jc * CH, CH)]).then_inc(stat_in[n], DMA)
                sp.dma_start(m_sb[n], m_dram[bass.ds(jc, 1), :, :].rearrange("g p w -> (g p) w")
                             ).then_inc(stat_in[n], DMA)

            for half in range(HALVES):
                load_q(half, 0)
            for n in range(PAIR):
                load_stationary(n, n * 0)
            with sp.Fori(0, NI) as rg:
                with sp.Fori(0, BODIES) as bd:
                    turn = rg * BODIES + bd
                    for ch in range(CHUNKS):
                        if ch == CHUNKS - 1:
                            with sp.If(bd > BODIES - 2):
                                with sp.If(rg < NI - 1):
                                    sp.wait_ge(logits_ready, turn * UNITS + ch * KT)
                                    load_q(0, (rg + 1) % NI)
                        sp.wait_ge(adjT_ready, turn * UNITS + (ch + 1) * KT)
                        next_chunk(sp, 0, turn, ch)
                        if ch % HALVES == HALVES - 1:
                            with sp.If(turn < TURNS - 1):
                                sp.wait_ge(agg_done, turn * UNITS + (ch + 1) * KT)
                                load_stationary(ch // HALVES, (turn + 1) % TURNS)
                with sp.If(rg < NI - 1):
                    load_q(1, (rg + 1) % NI)

            with sp.Fori(0, NJ) as g:
                sp.wait_ge(rows_ps, g)
                sp.dma_start(stage_d[:, :], xT_dram[:, bass.ds(g * CH, CH)]).then_inc(xs_in, DMA)
                sp.wait_ge(x1_rows, g + 1)
                sp.dma_start(x1_dram[bass.ds(g, 1), :, :].rearrange("g p w -> (g p) w"), stage_c[:, :]
                             ).then_inc(x1_out, DMA)
            sp.wait_ge(x1_out, NJ * DMA)
            sp.wait_ge(y_rows, NJ)
            sp.wait_ge(rows_ps, NJ)

            with sp.Fori(0, NI) as rg:
                for jj in range(HALVES):
                    if jj == 0:
                        sp.wait_ge(rows_done, HALVES * rg)
                    sp.dma_start((stage_c, stage_d)[jj][:, :],
                                 x1_dram[bass.ds(rg * HALVES + jj, 1), :, :].rearrange("g p w -> (g p) w")
                                 ).then_inc(x1_in, DMA)
                with sp.Fori(0, BODIES) as bd:
                    turn = rg * BODIES + bd
                    for ch in range(CHUNKS):
                        if ch + NAT < CHUNKS:
                            sp.wait_ge(adjT_ready, ALL + turn * UNITS + (ch + 1) * KT)
                            next_chunk(sp, 0, turn, ch)
                        else:
                            with sp.If(turn < TURNS - 1):
                                sp.wait_ge(adjT_ready, ALL + turn * UNITS + (ch + 1) * KT)
                                next_chunk(sp, 0, turn, ch)
                for jj in range(HALVES):
                    sp.wait_ge(rows_done, HALVES * rg + jj + 1)
                    for a in range(A):
                        dst = out[bass.ds(rg * RANGE + jj * CH + a * (CH // A), CH // A), :]
                        sp.dma_start(dst.rearrange("(k r) d -> r k d", r=BLK),
                                     by_slot(stage_b[a * BLK:(a + 1) * BLK, :])).then_inc(out_done, DMA)
            sp.wait_ge(out_done, NJ * A * DMA)

        @block.gpsimd
        def _(pool):
            nc.gpsimd.memset(ident[:, :], 0.0).then_inc(made, 1)
            nc.gpsimd.memset(zeros[:, :], 0.0).then_inc(made, 1)
            nc.gpsimd.memset(ones[:, :], 1.0).then_inc(made, 1)
            nc.gpsimd.memset(ones_row[:, :], 1.0).then_inc(made, 1)
            nc.gpsimd.memset(eps_col[:, :], EPS).then_inc(made, 1)
            pool.wait_ge(made, 5)
            nc.gpsimd.affine_select(out=ident[:, :], in_=ident[:, :], compare_op=ALU.not_equal, fill=1.0,
                                    base=0, pattern=[[-1, P]], channel_multiplier=1).then_inc(made, 1)
            with pool.Fori(0, NI) as rg:
                with pool.Fori(0, BODIES) as bd:
                    turn = rg * BODIES + bd
                    for u in range(UNITS):
                        half = unit(u)[2]
                        part = degp[:, half * CH:(half + 1) * CH]
                        if u == 0:
                            pool.wait_ge(deg_clear, rg + 1)
                        pool.wait_ge(deg_added, turn * UNITS + u)
                        pool.wait_ge(adjT_ready, turn * UNITS + u + 1)
                        nc.gpsimd.tensor_tensor(stored(part), stored(part), permuted(adjT[u % ATB][:, :]),
                                                ALU.add).then_inc(deg_added, 1)

        @block.scalar
        def _(act):
            for ch in range(NAT):
                load_chunk(act, 1, 0, ch)
            act.wait_ge(const_loaded, 12 * DMA)
            act.wait_ge(made, 6)
            with act.Fori(0, NJ) as g:
                act.wait_ge(m_ps, g)
                act.wait_ge(mT_ps, g + 1)
                nc.scalar.activation(stage_c[:, :], lg[1][:, :], ACT.Identity, bias=bm_col[:, :]).then_inc(mT_ready, 1)
                act.wait_ge(stored_qk, 2 * DMA * g)
                act.wait_ge(qk_ps, 2 * g + 1)
                nc.scalar.activation(permuted(q_sb[:, 0, 0:CH]), stored(acc[:, 0:CH]), ACT.Copy).then_inc(qk_hi, 1)
                act.wait_ge(qk_ps, 2 * g + 2)
                nc.scalar.activation(k_sb[0][:, 0, :], acc[:, CH:2 * CH], ACT.Copy).then_inc(qk_hi, 1)
            with act.Fori(0, NI) as rg:
                with act.Fori(0, BODIES) as bd:
                    turn = rg * BODIES + bd
                    for u in range(UNITS):
                        at = turn * UNITS + u
                        act.wait_ge(gated_ready, at - 1 if u else at)
                        act.wait_ge(adjT_ready, at + 1)
                        nc.scalar.activation(sq[u % 2], adjT[u % ATB][:, :], ACT.Square).then_inc(sq_ready, 1)
                        act.wait_ge(logits_ready, at + 1)
                        nc.scalar.activation(lg[u % 2][:, :], lg[u % 2][:, :], ACT.Sigmoid, bias=gb_col[:, :],
                                             scale=float(D) ** -0.5).then_inc(probs_ready, 1)
                        if u % KT == KT - 1:
                            act.wait_ge(adjT_ready, at + 1)
                            next_chunk(act, 1, turn, u // KT)
                act.wait_ge(range_done, rg + 1)
                for half in range(HALVES):
                    last = nc.scalar.activation(stored(cols[:, bass.ds(rg * RANGE + half * CH, CH)]),
                                                permuted(acc[:, half * CH:(half + 1) * CH]), ACT.Copy)
                last.then_inc(acc_read, 1)
            act.wait_ge(deg_read, NI)
            nc.scalar.activation(root[:, :], deg[:, :], ACT.Sqrt).then_inc(root_ready, 1)
            with act.Fori(0, NJ) as g:
                act.wait_ge(rows_ps, g)
                act.wait_ge(upd_ps, g + 1)
                nc.scalar.activation(stage_a[:, :], lg[0][:, :], ACT.Relu, bias=bu_col[:, :]).then_inc(upd_ready, 1)
                for n in range(2):
                    act.wait_ge(var_ready, 2 * g + n + 1)
                    nc.scalar.activation(sd[:, :], mv[:, :, 1], ACT.Sqrt, bias=eps_col[:, :]).then_inc(sd_ready, 1)
                act.wait_ge(y_rows, g + 1)
                nc.scalar.activation(y_all[:, bass.ds(g * CH, CH)], stage_b[:, :], ACT.Copy).then_inc(y_kept, 1)
            def stage_y(n, turn):
                jc = (turn % BODIES) * PAIR + n
                nc.scalar.activation(y_sb[n][:, :], y_all[:, bass.ds(jc * CH, CH)], ACT.Copy).then_inc(y_staged, 1)

            act.wait_ge(y_kept, NJ)
            stage_y(0, 0)
            with act.Fori(0, NI) as rg:
                with act.Fori(0, BODIES) as bd:
                    turn = rg * BODIES + bd
                    for ch in range(CHUNKS):
                        if ch == 0:
                            act.wait_ge(hop_done, turn * UNITS)
                            stage_y(1, turn)
                        if ch == HALVES:
                            act.wait_ge(hop_done, turn * UNITS + HALVES * KT)
                            stage_y(0, (turn + 1) % TURNS)
                        if ch + NAT < CHUNKS:
                            act.wait_ge(adjT_ready, ALL + turn * UNITS + (ch + 1) * KT)
                            next_chunk(act, 1, turn, ch)
                        else:
                            with act.If(turn < TURNS - 1):
                                act.wait_ge(adjT_ready, ALL + turn * UNITS + (ch + 1) * KT)
                                next_chunk(act, 1, turn, ch)
                for jj in range(HALVES):
                    act.wait_ge(var_ready, 2 * NJ + HALVES * rg + jj + 1)
                    nc.scalar.activation(sd[:, :], mv[:, :, 1], ACT.Sqrt, bias=eps_col[:, :]).then_inc(sd_ready, 1)

        @block.tensor
        def _(pe):
            def open_sums():
                for b in range(RANGE // BANK):
                    nc.tensor.matmul(acc[:, b * BANK:(b + 1) * BANK], zeros[:, 0:P], zeros[:, :],
                                     start=True, stop=False)

            def close_sums():
                for b in range(RANGE // BANK):
                    last = nc.tensor.matmul(acc[:, b * BANK:(b + 1) * BANK], zeros[:, 0:P], zeros[:, :],
                                            start=False, stop=True)
                return last

            pe.wait_ge(const_loaded, 12 * DMA)
            pe.wait_ge(made, 6)
            nc.tensor.matmul(lg[0][:, 0:3 * D], ones_row[:, :], vec_rows[:, :], start=True, stop=True).then_inc(vec_ps, 1)
            pe.wait_ge(vec_done, 1)
            with pe.Fori(0, NJ) as g:
                pe.wait_ge(x_in, (g + 1) * DMA)
                pe.wait_ge(m_ready, g)
                for k in range(KT):
                    last = nc.tensor.transpose(lg[0][:, k * P:(k + 1) * P], stage_a[:, k * P:(k + 1) * P], ident[:, :])
                last.then_inc(xT_ps, 1)
                pe.wait_ge(xT_ready, g + 1)
                pe.wait_ge(mT_ready, g)
                for s in banks(0):
                    last = nc.tensor.matmul(lg[1][:, s], w_msg[:, :], stage_b[:, s], start=True, stop=True)
                last.then_inc(mT_ps, 1)
                pe.wait_ge(mT_ready, g + 1)
                pe.wait_ge(qk_lo, 2 * g)
                for w, half in ((w_q, 0), (w_k, 1)):
                    for s, t in zip(banks(half), banks(0)):
                        last = nc.tensor.matmul(acc[:, s], w[:, :], stage_c[:, t], start=True, stop=True)
                    last.then_inc(qk_ps, 1)
                for k in range(KT):
                    last = nc.tensor.transpose(lg[0][:, k * P:(k + 1) * P], stage_c[:, k * P:(k + 1) * P], ident[:, :])
                last.then_inc(m_ps, 1)

            def logits(u):
                _, n, half, k = unit(u)
                for s, t in zip(banks(half), banks(0)):
                    for kp, qp in ((0, 0), (0, 1), (1, 0)):
                        last = nc.tensor.matmul(lg[u % 2][:, t], k_sb[n][:, kp, k * P:(k + 1) * P], q_sb[:, qp, s],
                                                start=(kp == 0 and qp == 0), stop=(kp == 1))
                last.then_inc(logits_ready, 1)

            def aggregate(u):
                _, n, half, k = unit(u)
                for s, t in zip(banks(half), banks(0)):
                    last = nc.tensor.matmul(acc[:, s], m_sb[n][:, k * P:(k + 1) * P], gated[u % 2][:, t],
                                            start=False, stop=False)
                last.then_inc(agg_done, 1)

            pe.wait_ge(m_ready, NJ)
            pe.wait_ge(qk_lo, 2 * NJ)
            pe.wait_ge(q_in[0], DMA)
            pe.wait_ge(stat_in[0], 2 * DMA)
            logits(0)
            with pe.Fori(0, NI) as rg:
                pe.wait_ge(deg_read, rg)
                open_sums()
                with pe.Fori(0, BODIES) as bd:
                    turn = rg * BODIES + bd
                    for u in range(UNITS):
                        at = turn * UNITS + u
                        if u + 1 < UNITS:
                            _, n, half, k = unit(u + 1)
                            if k == 0 and n == 0:
                                pe.wait_ge(q_in[half], (rg + 1) * DMA)
                            if k == 0 and half == 0:
                                pe.wait_ge(stat_in[n], (turn + 1) * 2 * DMA)
                            pe.wait_ge(gated_ready, at)
                            logits(u + 1)
                        else:
                            with pe.If(turn < TURNS - 1):
                                pe.wait_ge(q_in[0], ((turn + 1) // BODIES + 1) * DMA)
                                pe.wait_ge(stat_in[0], (turn + 2) * 2 * DMA)
                                pe.wait_ge(gated_ready, at)
                                logits(0)
                        pe.wait_ge(gated_ready, at + 1)
                        aggregate(u)
                close_sums().then_inc(range_done, 1)
                pe.wait_ge(acc_read, rg + 1)
                pe.wait_ge(deg_added, (rg + 1) * BODIES * UNITS)
                for jj in range(HALVES):
                    for k in range(KT):
                        t = jj * KT + k
                        last = nc.tensor.matmul(acc[:, t:t + 1], degp[:, t * P:(t + 1) * P],
                                                ones[:, :], start=True, stop=True)
                last.then_inc(deg_ps, 1)

            pe.wait_ge(deg_read, NI)
            with pe.Fori(0, NJ) as g:
                pe.wait_ge(xs_in, (g + 1) * DMA)
                pe.wait_ge(upd_ready, g)
                for b, s in enumerate(banks(0)):
                    nc.tensor.matmul(lg[0][:, s], w_ut[:, :], stage_d[:, s], start=True, stop=False)
                    last = nc.tensor.matmul(lg[0][:, s], w_ub[:, :], cols[:, bass.ds(g * CH + b * BANK, BANK)],
                                            start=False, stop=True)
                last.then_inc(upd_ps, 1)
                pe.wait_ge(upd_ready, g + 1)
                pe.wait_ge(y_rows, g)
                for src, dst in ((stage_a, lg[1]), (stage_d, acc)):
                    for k in range(KT):
                        last = nc.tensor.transpose(dst[:, k * P:(k + 1) * P], src[:, k * P:(k + 1) * P], ident[:, :])
                last.then_inc(rows_ps, 1)
                pe.wait_ge(y_rows, g + 1)
                pe.wait_ge(yT_ready, g)
                for k in range(KT):
                    last = nc.tensor.transpose(acc[:, CH + k * P:CH + (k + 1) * P], stage_b[:, k * P:(k + 1) * P],
                                               ident[:, :])
                last.then_inc(yT_ps, 1)

            pe.wait_ge(yT_ready, NJ)
            with pe.Fori(0, NI) as rg:
                open_sums()
                with pe.Fori(0, BODIES) as bd:
                    turn = rg * BODIES + bd
                    for u in range(UNITS):
                        _, n, half, k = unit(u)
                        if k == 0 and half == 0:
                            pe.wait_ge(y_staged, turn * PAIR + n + 1)
                        pe.wait_ge(adjT_ready, ALL + turn * UNITS + u + 1)
                        for s, t in zip(banks(half), banks(0)):
                            last = nc.tensor.matmul(acc[:, s], y_sb[n][:, k * P:(k + 1) * P], adjT[u % ATB][:, t],
                                                    start=False, stop=False)
                        last.then_inc(hop_done, 1)
                close_sums().then_inc(hop_range, 1)
                pe.wait_ge(s_ready, rg + 1)
                for jj in range(HALVES):
                    pe.wait_ge(rows_done, HALVES * rg)
                    for k in range(KT):
                        last = nc.tensor.matmul(lg[jj][:, k * P:(k + 1) * P],
                                                sT[:, jj * CH + k * P:jj * CH + (k + 1) * P], w_1[:, :],
                                                start=True, stop=True)
                    last.then_inc(z_ps, 1)

        @block.vector
        def _(dve):
            def transpose(u):
                _, _, _, k = unit(u % UNITS)
                ch = (u // KT) % CHUNKS
                nc.vector.transpose(adjT[u % ATB][:, :].rearrange("p (c s) -> p c s", s=BLK),
                                    nat[ch % NAT][:, :, k * BLK:(k + 1) * BLK]).then_inc(adjT_ready, 1)

            def wait_chunk(turns, ch):
                for who in range(2):
                    dve.wait_ge(nat_in[ch % NAT][who], (turns * (CHUNKS // NAT) + ch // NAT + 1) * 2 * DMA)

            def next_transpose(turns, u):
                v = u + ATB
                if v % KT == 0:
                    if v < UNITS:
                        wait_chunk(turns, v // KT)
                    else:
                        wait_chunk(turns + 1, 0)
                transpose(v)

            dve.wait_ge(vec_ps, 1)
            nc.vector.tensor_copy(vec_all[:, :, :].rearrange("p a d -> p (a d)"), lg[0][:, 0:3 * D]).then_inc(vec_done, 1)
            with dve.Fori(0, NJ) as g:
                dve.wait_ge(stored_x, g * DMA)
                dve.wait_ge(xT_ps, g + 1)
                nc.vector.tensor_copy(stored(stage_b[:, :]), permuted(lg[0][:, :])).then_inc(xT_ready, 1)
                dve.wait_ge(qk_hi, 2 * g + 1)
                nc.vector.tensor_tensor(permuted(q_sb[:, 1, 0:CH]), stored(acc[:, 0:CH]),
                                        permuted(q_sb[:, 0, 0:CH].bitcast(F32)), ALU.subtract).then_inc(qk_lo, 1)
                dve.wait_ge(qk_hi, 2 * g + 2)
                nc.vector.tensor_tensor(k_sb[0][:, 1, :], acc[:, CH:2 * CH], k_sb[0][:, 0, :].bitcast(F32),
                                        ALU.subtract).then_inc(qk_lo, 1)
                dve.wait_ge(stored_m, g * DMA)
                dve.wait_ge(m_ps, g + 1)
                nc.vector.tensor_copy(stage_d[:, :], lg[0][:, :]).then_inc(m_ready, 1)

            nc.vector.memset(degp, 0.0).then_inc(deg_clear, 1)
            wait_chunk(0, 0)
            for u in range(ATB):
                transpose(u)
            with dve.Fori(0, NI) as rg:
                with dve.Fori(0, BODIES) as bd:
                    turn = rg * BODIES + bd
                    for u in range(UNITS):
                        at = turn * UNITS + u
                        dve.wait_ge(sq_ready, at + 1)
                        dve.wait_ge(probs_ready, at + 1)
                        nc.vector.tensor_tensor(gated[u % 2], lg[u % 2][:, :], sq[u % 2], ALU.mult).then_inc(gated_ready, 1)
                        dve.wait_ge(deg_added, at + 1)
                        next_transpose(turn, u)
                dve.wait_ge(deg_ps, rg + 1)
                nc.vector.tensor_scalar(deg[:, bass.ds(rg * HALVES * KT, HALVES * KT)], acc[:, 0:HALVES * KT],
                                        1.0, None, ALU.add).then_inc(deg_read, 1)
                nc.vector.memset(degp, 0.0).then_inc(deg_clear, 1)

            done = [0]

            def link(last, base):
                done[0] += 1
                last.then_inc(step, 1)
                dve.wait_ge(step, base + done[0])

            def normalise(dst, src, base, norms):
                for k in range(KT):
                    last = nc.vector.bn_stats(stats[:, k, :], src[:, k * P:(k + 1) * P])
                nc.vector.drain()
                for k in range(KT):
                    last = nc.vector.bn_aggr(mv[:, k, :], stats[:, k, :])
                last.then_inc(var_ready, 1)
                dve.wait_ge(sd_ready, norms + 1)
                link(nc.vector.reciprocal(rstd[:, :], sd[:, :]), base)
                for k in range(KT):
                    last = nc.vector.tensor_scalar(dst[:, k * P:(k + 1) * P], src[:, k * P:(k + 1) * P],
                                                   mv[:, k, 0:1], rstd[:, k:k + 1], ALU.subtract, ALU.mult)
                return last

            def each_row(v):
                return vec_all[:, v:v + 1, :].to_broadcast([P, KT, D])

            dve.wait_ge(root_ready, 1)
            nc.vector.reciprocal(dinv[:, :], root[:, :]).then_inc(dinv_ready, 1)
            dve.wait_ge(dinv_ready, 1)
            MID = 6
            with dve.Fori(0, NJ) as g:
                done[0] = 0
                base = g * MID
                dve.wait_ge(rows_ps, g + 1)
                dve.wait_ge(y_kept, g)
                dve.wait_ge(yT_ps, g)
                link(normalise(stage_b, lg[1], base, 2 * g), base)
                link(nc.vector.tensor_tensor(by_slot(stage_b[:, :]), by_slot(stage_b[:, :]), each_row(0), ALU.mult), base)
                link(nc.vector.tensor_tensor(by_slot(stage_b[:, :]), by_slot(stage_b[:, :]), each_row(1), ALU.add), base)
                link(nc.vector.tensor_tensor(stage_b[:, :], stage_b[:, :], acc[:, 0:CH], ALU.add), base)
                dve.wait_ge(x1_out, g * DMA)
                last = normalise(stage_c, stage_b, base, 2 * g + 1)
                last.then_inc(x1_rows, 1)
                dve.wait_ge(x1_rows, g + 1)
                for k in range(KT):
                    last = nc.vector.tensor_scalar(stage_b[:, k * P:(k + 1) * P], stage_c[:, k * P:(k + 1) * P],
                                                   dinv[:, bass.ds(g * KT + k, 1)], None, ALU.mult)
                last.then_inc(y_rows, 1)
                dve.wait_ge(yT_ps, g + 1)
                nc.vector.tensor_copy(cols[:, bass.ds(g * CH, CH)], acc[:, CH:2 * CH]).then_inc(yT_ready, 1)
                assert done[0] == MID

            FIN = 4
            with dve.Fori(0, NI) as rg:
                with dve.Fori(0, BODIES) as bd:
                    turn = rg * BODIES + bd
                    for u in range(UNITS):
                        if u + ATB < UNITS:
                            dve.wait_ge(hop_done, turn * UNITS + u + 1)
                            next_transpose(TURNS + turn, u)
                        else:
                            with dve.If(turn < TURNS - 1):
                                dve.wait_ge(hop_done, turn * UNITS + u + 1)
                                next_transpose(TURNS + turn, u)
                dve.wait_ge(hop_range, rg + 1)
                dve.wait_ge(z_ps, HALVES * rg)
                for half in range(HALVES):
                    part = slice(half * CH, (half + 1) * CH)
                    last = nc.vector.tensor_tensor(stored(sT[:, part]), permuted(acc[:, part]),
                                                   stored(cols[:, bass.ds(rg * RANGE + half * CH, CH)]), ALU.add)
                last.then_inc(s_ready, 1)
                for jj in range(HALVES):
                    done[0] = 0
                    base = NJ * MID + (rg * HALVES + jj) * FIN
                    z, x1 = lg[jj], (stage_c, stage_d)[jj]
                    dve.wait_ge(rows_done, HALVES * rg + jj)
                    dve.wait_ge(z_ps, HALVES * rg + jj + 1)
                    for k in range(KT):
                        last = nc.vector.tensor_scalar(stage_a[:, k * P:(k + 1) * P], z[:, k * P:(k + 1) * P],
                                                       dinv[:, bass.ds((rg * HALVES + jj) * KT + k, 1)], None, ALU.mult)
                    link(last, base)
                    link(nc.vector.tensor_tensor(by_slot(stage_a[:, :]), by_slot(stage_a[:, :]), each_row(2), ALU.add), base)
                    dve.wait_ge(x1_in, (rg * HALVES + HALVES) * DMA)
                    link(nc.vector.scalar_tensor_tensor(out=stage_a[:, :], in0=stage_a[:, :], scalar=0.0,
                                                        in1=x1[:, :], op0=ALU.max, op1=ALU.add), base)
                    dve.wait_ge(out_done, (rg * HALVES + jj) * A * DMA)
                    last = normalise(stage_b, stage_a, base, 2 * NJ + rg * HALVES + jj)
                    last.then_inc(rows_done, 1)
                    assert done[0] == FIN


_INS = ['x', 'adj', 'L0_gnn_W_msg', 'L0_gnn_b_msg', 'L0_gnn_W_q', 'L0_gnn_W_k', 'L0_gnn_gate_bias',
        'L0_gnn_W_upd', 'L0_gnn_b_upd', 'L0_gnn_ln_gamma', 'L0_gnn_ln_beta', 'L1_gnn_W', 'L1_gnn_b']


def kernel(**inputs):
    import numpy as _np
    import concourse.bacc as _bacc
    from concourse import mybir as _mybir
    from concourse.bass_utils import run_bass_kernel_spmd as _run

    nc = _bacc.Bacc("TRN2", target_bir_lowering=False, num_devices=1)
    arrays, args = {}, []
    for name in _INS:
        a = _np.ascontiguousarray(inputs[name])
        if a.ndim == 0:
            a = a.reshape(1)
        arrays[f"in_{name}"] = a
        args.append(nc.dram_tensor(f"in_{name}", a.shape, _mybir.dt.from_np(a.dtype), kind="ExternalInput").ap())
    args.append(nc.dram_tensor("out_0", (N, D), F32, kind="ExternalOutput").ap())
    build(nc, *args)
    r = _run(nc, [arrays], core_ids=[0])
    return r.results[0]["out_0"]
```

```python
import concourse.bass as bass
from concourse import mybir
from contextlib import ExitStack

F32 = mybir.dt.float32
F32R = mybir.dt.float32r
BF16 = mybir.dt.bfloat16
ALU = mybir.AluOpType
ACT = mybir.ActivationFunctionType

N, D = 8192, 128
P = 128
BLK = 32
CH = 1024
BANK = 512
RANGE = 2048
NJ = N // CH
NI = N // RANGE
A = P // BLK
KT = CH // P
V = KT // 2
C = BANK // BLK
QUARTERS = RANGE // BANK
HALVES = RANGE // CH
PAIR = 2
BODIES = NJ // PAIR
CHUNKS = PAIR * QUARTERS
UNITS = CHUNKS * V
NAT = 4
ATB = 8
HT = KT // 2
PIECE = HT * P
EPS = 1e-5
DMA = 16
START = 8
MIDS = dict(norm1=1, beta=1, stat2=3, norm2=6, root1=7, root2=12, keep=15,
            upd=10, relu=15, rows=14, stat1=15)
STAGE = (5, 21)
TAIL = NI * BODIES - BODIES
LAST = dict(copy=3, z=2, stat=4, root=10, norm=8)


def build(nc, x, adj, W_msg, b_msg, W_q, W_k, gate_bias, W_upd, b_upd, ln_gamma, ln_beta, W1, b1, out):
    q_dram = nc.dram_tensor("q_split", (P, 2, N), F32, kind="Internal").ap()
    k_dram = nc.dram_tensor("k_split", (P, 2, N), F32, kind="Internal").ap()
    m_dram = nc.dram_tensor("messages", (NJ, P, CH), F32, kind="Internal").ap()
    agg_dram = nc.dram_tensor("aggregated", (P, N), F32, kind="Internal").ap()
    xT_dram = nc.dram_tensor("x_transposed", (P, N), F32, kind="Internal").ap()
    x1_dram = nc.dram_tensor("x_layer1", (2 * NJ, P, PIECE), F32, kind="Internal").ap()

    ctx = ExitStack()
    with ctx:
        def sb(name, shape, dt=F32):
            return ctx.enter_context(nc.sbuf_tensor(name, shape, dt))

        def sem(name):
            return ctx.enter_context(nc.semaphore(name))

        nat = [sb(f"nat{n}", [P, C, CH // A]) for n in range(NAT)]
        adjT = [sb(f"adjT{n}", [P, CH]) for n in range(ATB)]
        q_sb = sb("q_sb", [P, 2, RANGE], F32R)
        k_sb = [sb(f"k_sb{n}", [P, 2, CH], F32R) for n in range(PAIR)]
        split_sb = sb("split_sb", [P, 2, CH], F32R)
        adj_hi = [q_sb[:, 0, n * CH:(n + 1) * CH] for n in range(2)] + [k_sb[n][:, 1, :] for n in range(2)]
        adj_lo = [q_sb[:, 1, n * CH:(n + 1) * CH] for n in range(2)] + [split_sb[:, n, :] for n in range(2)]
        y_hi, y_lo = ([k_sb[n][:, 0, part * PIECE:(part + 1) * PIECE] for n in range(PAIR)] for part in range(2))
        y_sb = [sb(f"y_sb{n}", [P, PIECE]) for n in range(PAIR)]
        work = sb("work", [P, 4, 2 * CH])
        sq = [work[:, 0, n * CH:(n + 1) * CH] for n in range(2)]
        gated = [work[:, 1, n * CH:(n + 1) * CH] for n in range(2)]
        m_sb = [work[:, 2, n * CH:(n + 1) * CH] for n in range(PAIR)]
        degp = work[:, 3, :]
        y_all = work[:, :, :].rearrange("p a b -> p (a b)")
        mT_sb, xT_sb = ([adjT[n + p][:, :] for p in range(2)] for n in (4, 6))
        sT = sb("sT", [P, RANGE])
        agg_col = sb("agg_col", [P, CH])
        x_col = sb("x_col", [P, CH])
        u_col = sT[:, 0:CH]
        stage_a = sb("stage_a", [P, CH])
        stage_b = sb("stage_b", [P, CH])
        stage_c = sb("stage_c", [P, CH])
        x_rows = [stage_a, stage_b]
        x_res, n_rows, x1_sb = stage_a[:, :], stage_b[:, :], stage_c[:, :]
        res, z_rows, results = ([t[:, n * PIECE:(n + 1) * PIECE] for n in range(2)]
                                for t in (stage_a, stage_b, stage_c))
        s_piece = x_col[:, 0:PIECE]
        ident = sb("ident", [P, P])
        ident_r = sb("ident_r", [P, P], F32R)
        zeros = sb("zeros", [P, BANK], BF16)
        ones = sb("ones", [P, 1])
        w_ut, w_ub, w_1 = (sb(n, [P, D]) for n in ("w_ut", "w_ub", "w_1"))
        w_msg, w_q, w_k = (sT[:, n * D:(n + 1) * D] for n in range(3))
        vec_rows = sT[0:1, CH:CH + 3 * D]
        ones_row = sT[0:1, CH + 3 * D:CH + 3 * D + P]
        bm_col, bu_col, gb_col, eps_col, one_col = (sb(n, [P, 1]) for n in
                                                    ("bm_col", "bu_col", "gb_col", "eps_col", "one_col"))
        vec_all = sb("vec_all", [P, 3, D])
        deg = sb("deg", [P, NJ * KT])
        root = sb("root", [P, NJ * KT])
        dinv = sb("dinv", [P, NJ * KT])
        dinv_now = sb("dinv_now", [P, KT])
        stats = sb("stats", [P, KT, 6])
        mv = sb("mv", [P, KT, 2])
        sd = sb("sd", [P, KT])
        rstd = sb("rstd", [P, KT])

        acc = ctx.enter_context(nc.psum_tensor("acc", [P, RANGE], F32))
        lg = [ctx.enter_context(nc.psum_tensor(f"lg{n}", [P, CH], F32)) for n in range(2)]

        def sems(*names):
            return [sem(n) for n in names]

        (const_loaded,) = sems("const_loaded")
        kept = sems("kept0", "kept1")
        x_in = sems("x_in0", "x_in1")
        q_in = sems(*[f"q_in{h}" for h in range(HALVES)])
        stat_in = sems(*[f"stat_in{n}" for n in range(PAIR)])
        nat_in = [sems(f"nat_in{n}_sp", f"nat_in{n}_act") for n in range(NAT)]
        x_col_in, x_res_in, x1_out = sems("x_col_in", "x_res_in", "x1_out")
        (agg_out,) = sems("agg_out")
        res_in, out_done = sems("res_in0", "res_in1"), sems("out_done0", "out_done1")

        started = {}

        def counted_by(engine, *names):
            started.setdefault(engine, []).extend(sems(*names))
            return started[engine][-len(names):]

        def start(engine, eng):
            for s in started[engine]:
                eng.sem_inc(s, START)

        (made,), (vec_ps,), (vec_done,) = (counted_by("pool", "made"), counted_by("pe", "vec_ps"),
                                           counted_by("dve", "vec_done"))
        (scratched,) = counted_by("sp", "scratched")
        mT_ready, qk_hi = counted_by("act", "mT_ready", "qk_hi")
        xT_ps, mT_ps, qk_ps, m_ps = counted_by("pe", "xT_ps", "mT_ps", "qk_ps", "m_ps")
        xT_ready, qk_lo, m_ready = counted_by("dve", "xT_ready", "qk_lo", "m_ready")
        adjT_ready, gated_ready = counted_by("dve", "adjT_ready", "gated_ready")
        sq_ready, probs_ready = counted_by("act", "sq_ready", "probs_ready")
        logits_ready, agg_done = counted_by("pe", "logits_ready", "agg_done")
        (deg_added,) = counted_by("pool", "deg_added")
        range_done, deg_ps = counted_by("pe", "range_done", "deg_ps")
        (acc_read,), (agg_kept,) = counted_by("act", "acc_read"), counted_by("sp", "agg_kept")
        deg_read, deg_clear = counted_by("dve", "deg_read", "deg_clear")
        root_ready, upd_ready, y_rows = counted_by("act", "root_ready", "upd_ready", "y_rows")
        upd_ps, rows_ps = counted_by("pe", "upd_ps", "rows_ps")
        dinv_ready, res_added, x1_rows = counted_by("dve", "dinv_ready", "res_added", "x1_rows")
        (beta_added,) = counted_by("pool", "beta_added")
        (x1_kept,) = counted_by("sp", "x1_kept")
        var_ready, step = counted_by("dve", "var_ready", "step")
        (sd_ready,) = counted_by("act", "sd_ready")
        y_staged, hi_ready, s_half0, s_piece_in = counted_by("act", "y_staged", "hi_ready", "s_half0", "s_piece_in")
        y_split, lo_ready = counted_by("pool", "y_split", "lo_ready")
        hop_done, hop_range, z_ps = counted_by("pe", "hop_done", "hop_range", "z_ps")
        s_half1, res_used, rows_done = counted_by("dve", "s_half1", "res_used", "rows_done")
        (out_free,) = counted_by("sp", "out_free")

        z_bank = [lg[n // 2][:, n % 2 * PIECE:(n % 2 + 1) * PIECE] for n in range(BODIES)]

        block = ctx.enter_context(nc.Block())

        TURNS = NI * BODIES
        ALL = TURNS * UNITS

        def permuted(t):
            return t.rearrange("p (a k r) -> p k a r", a=A, k=KT)

        def stored(t):
            return t.rearrange("p (k a r) -> p k a r", a=A, k=KT)

        def by_slot(t):
            return t.rearrange("p (k d) -> p k d", k=KT)

        def nth(n):
            return n + START

        def load_chunk(eng, who, turn, ch):
            i0 = (turn // BODIES) * RANGE + (ch % QUARTERS) * BANK
            j0 = (turn % BODIES) * (PAIR * CH) + (ch // QUARTERS) * CH
            for a in (2 * who, 2 * who + 1):
                src = adj[bass.ds(i0, BANK), bass.ds(j0 + a * (CH // A), CH // A)]
                eng.dma_start(nat[ch % NAT][a * BLK:(a + 1) * BLK, :, :],
                              src.rearrange("(c s) w -> s c w", s=BLK)).then_inc(nat_in[ch % NAT][who], DMA)

        def next_chunk(eng, who, turn, ch):
            if ch + NAT < CHUNKS:
                load_chunk(eng, who, turn, ch + NAT)
            else:
                load_chunk(eng, who, (turn + 1) % TURNS, ch + NAT - CHUNKS)

        def unit(u):
            ch = u // V
            return ch, ch // QUARTERS, ch % QUARTERS, u % V

        def bank(b):
            return slice(b * BANK, (b + 1) * BANK)

        def tile_at(k):
            return slice(k * P, (k + 1) * P)

        def of_units(y, split):
            return y.rearrange("p (w s t) -> p w s t", s=2, t=2 * P)[:, :, split, :]

        @block.sync
        def _(sp):
            start("sp", sp)
            sp.sem_inc(scratched, 1)

            def load_x(p, g):
                sp.dma_start(by_slot(x_rows[p][:, :]),
                             x[bass.ds(g * CH, CH), :].rearrange("(k p) d -> p k d", p=P)).then_inc(x_in[p], DMA)

            def stored_by(p, stores):
                sp.wait_ge(kept[p], stores * DMA)
                sp.sem_inc(scratched, 1)

            def prologue(h, pair, following):
                for p in range(2):
                    n, g = 2 * pair + p, 2 * h + p
                    sp.wait_ge(xT_ready, nth(n + 1))
                    if following is not None:
                        load_x(p, following + p)
                    sp.dma_start(xT_dram[:, bass.ds(g * CH, CH)], xT_sb[p]).then_inc(kept[p], DMA)
                    if p == 1:
                        stored_by(0, pair * 4 + (3 if following is None else 4))
                    elif isinstance(pair, int):
                        stored_by(1, pair * 4)
                    else:
                        with sp.If(pair != 0):
                            stored_by(1, pair * 4)
                    sp.wait_ge(qk_lo, nth(2 * n + 2))
                    if following is not None:
                        sp.dma_start(q_dram[:, :, bass.ds(g * CH, CH)], q_sb[:, :, p * CH:(p + 1) * CH].bitcast(F32)
                                     ).then_inc(kept[p], DMA)
                    sp.dma_start(k_dram[:, :, bass.ds(g * CH, CH)], k_sb[p][:, :, :].bitcast(F32)
                                 ).then_inc(kept[p], DMA)
                    sp.wait_ge(m_ready, nth(n + 1))
                    sp.dma_start(m_dram[bass.ds(g, 1), :, :].rearrange("g p w -> (g p) w"), m_sb[p]
                                 ).then_inc(kept[p], DMA)

            load_x(0, 2)
            load_x(1, 3)
            for dst, src in ((w_msg, W_msg), (w_q, W_q), (w_k, W_k), (w_1, W1),
                             (w_ut, W_upd[0:D, :]), (w_ub, W_upd[D:2 * D, :])):
                sp.dma_start(dst[:, :], src).then_inc(const_loaded, DMA)
            for dst, src in ((bm_col, b_msg), (bu_col, b_upd)):
                sp.dma_start(dst[:, :], src.rearrange("(d o) -> d o", o=1)).then_inc(const_loaded, DMA)
            sp.dma_start(gb_col[:, :], gate_bias.rearrange("(a b) -> a b", b=1).to_broadcast([P, 1])
                         ).then_inc(const_loaded, DMA)
            for n, src in enumerate((ln_gamma, ln_beta, b1)):
                sp.dma_start(vec_rows[:, n * D:(n + 1) * D], src.rearrange("(a d) -> a d", a=1)
                             ).then_inc(const_loaded, DMA)
            with sp.Fori(1, NJ // 2 - 1) as h:
                prologue(h, h - 1, 2 * h + 2)
            prologue(NJ // 2 - 1, NJ // 2 - 2, 0)
            prologue(0, NJ // 2 - 1, None)
            stored_by(1, (NJ // 2 - 1) * 4 + 3)

            def load_q(half, rg):
                sp.dma_start(q_sb[:, :, half * CH:(half + 1) * CH].bitcast(F32),
                             q_dram[:, :, bass.ds(rg * RANGE + half * CH, CH)]).then_inc(q_in[half], DMA)

            def load_stationary(n, turn):
                jc = (turn % BODIES) * PAIR + n
                sp.dma_start(k_sb[n][:, :, :].bitcast(F32), k_dram[:, :, bass.ds(jc * CH, CH)]).then_inc(stat_in[n], DMA)
                sp.dma_start(m_sb[n], m_dram[bass.ds(jc, 1), :, :].rearrange("g p w -> (g p) w")
                             ).then_inc(stat_in[n], DMA)

            def load_cols(g):
                sp.wait_ge(upd_ps, nth(g))
                sp.dma_start(x_col[:, :], xT_dram[:, bass.ds(g * CH, CH)]).then_inc(x_col_in, DMA)
                sp.dma_start(agg_col[:, :], agg_dram[:, bass.ds(g * CH, CH)]).then_inc(x_col_in, DMA)

            with sp.Fori(0, NI) as rg:
                with sp.Fori(0, BODIES) as bd:
                    turn = rg * BODIES + bd
                    for ch in range(CHUNKS):
                        if ch == CHUNKS - 2:
                            with sp.If(bd > BODIES - 2):
                                with sp.If(rg < NI - 1):
                                    sp.wait_ge(logits_ready, nth(turn * UNITS + ch * V))
                                    load_q(0, (rg + 1) % NI)
                        sp.wait_ge(adjT_ready, nth(turn * UNITS + (ch + 1) * V))
                        next_chunk(sp, 0, turn, ch)
                        if ch % QUARTERS == QUARTERS - 1:
                            with sp.If(turn < TURNS - 1):
                                sp.wait_ge(agg_done, nth(turn * UNITS + (ch + 1) * V))
                                load_stationary(ch // QUARTERS, (turn + 1) % TURNS)
                with sp.If(rg < NI - 1):
                    sp.wait_ge(logits_ready, nth((rg + 1) * BODIES * UNITS))
                    load_q(1, (rg + 1) % NI)
                with sp.If(rg > NI - 2):
                    load_cols(0)
                sp.wait_ge(acc_read, nth(rg + 1))
                sp.dma_start(agg_dram[:, bass.ds(rg * RANGE, RANGE)], sT[:, :]).then_inc(agg_out, DMA)
                sp.wait_ge(agg_out, (rg + 1) * DMA)
                sp.sem_inc(agg_kept, 1)

            def load_x_res(g):
                sp.wait_ge(res_added, nth(g))
                for a in range(A):
                    src = x[bass.ds(g * CH + a * (CH // A), CH // A), :].rearrange("(k r) d -> r k d", r=BLK)
                    sp.dma_start(by_slot(stage_a[a * BLK:(a + 1) * BLK, :]), src).then_inc(x_res_in, DMA)

            def store_x1(g):
                sp.wait_ge(x1_rows, nth(g + 1))
                sp.dma_start(x1_dram[bass.ds(2 * g, 2), :, :].rearrange("h p w -> p h w"),
                             x1_sb.rearrange("p (h w) -> p h w", h=2)).then_inc(x1_out, DMA)

            def x1_stored(g):
                sp.wait_ge(x1_out, (g + 1) * DMA)
                sp.sem_inc(x1_kept, 1)

            def chunk(turn, ch):
                sp.wait_ge(adjT_ready, nth(ALL + turn * UNITS + (ch + 1) * V))
                next_chunk(sp, 0, turn, ch)

            load_x_res(0)
            load_cols(1)
            load_x_res(1)
            store_x1(0)
            x1_stored(0)
            with sp.Fori(0, BODIES - 1) as bd:
                for ch in range(CHUNKS):
                    g = 2 * bd + 1 + ch // QUARTERS
                    if ch % QUARTERS == 1:
                        load_cols(g + 1)
                    if ch % QUARTERS == 2:
                        load_x_res(g + 1)
                    chunk(bd, ch)
                    if ch % QUARTERS == QUARTERS - 1:
                        store_x1(g)
                        x1_stored(g)
            for ch in range(CHUNKS):
                chunk(BODIES - 1, ch)
                if ch == QUARTERS - 1:
                    store_x1(NJ - 1)
                    x1_stored(NJ - 1)

            def load_res(piece, at=0):
                sp.dma_start(res[at], x1_dram[bass.ds(piece, 1), :, :].rearrange("h p w -> (h p) w")
                             ).then_inc(res_in[at], DMA)

            def store_results(piece, at=0):
                sp.wait_ge(rows_done, nth(piece + 1))
                for a in range(A):
                    row = (piece // 2) * CH + (piece % 2) * (HT * BLK) + a * (CH // A)
                    dst = out[bass.ds(row, HT * BLK), :].rearrange("(k r) d -> r k d", r=BLK)
                    sp.dma_start(dst, results[at][a * BLK:(a + 1) * BLK, :].rearrange("p (k d) -> p k d", k=HT)
                                 ).then_inc(out_done[at], DMA)

            sp.wait_ge(res_added, nth(NJ))
            load_res(0)
            with sp.Fori(1, NI) as rg:
                with sp.Fori(0, BODIES) as bd:
                    turn = rg * BODIES + bd
                    piece = turn - BODIES
                    for ch in range(CHUNKS):
                        if ch == 3:
                            store_results(piece)
                            load_res(piece + 1)
                        if ch + NAT < CHUNKS:
                            chunk(turn, ch)
                        else:
                            with sp.If(turn < TURNS - 1):
                                chunk(turn, ch)
                        if ch == CHUNKS - 1:
                            sp.wait_ge(out_done[0], (piece + 1) * A * DMA)
                            sp.sem_inc(out_free, 1)
            load_res(TAIL + 1, 1)
            for n in range(BODIES):
                store_results(TAIL + n, n % 2)
                if n + 2 < BODIES:
                    load_res(TAIL + n + 2, n % 2)
                    sp.wait_ge(out_done[n % 2], ((TAIL if n % 2 == 0 else 0) + n // 2 + 1) * A * DMA)
                    sp.sem_inc(out_free, 1)
            sp.wait_ge(out_done[0], (TAIL + 2) * A * DMA)
            sp.wait_ge(out_done[1], 2 * A * DMA)

        @block.gpsimd
        def _(pool):
            start("pool", pool)
            nc.gpsimd.memset(ident[:, :], 0.0).then_inc(made, 1)
            nc.gpsimd.memset(zeros[:, :], 0.0).then_inc(made, 1)
            nc.gpsimd.memset(ones[:, :], 1.0).then_inc(made, 1)
            nc.gpsimd.memset(ones_row, 1.0).then_inc(made, 1)
            nc.gpsimd.memset(eps_col[:, :], EPS).then_inc(made, 1)
            pool.wait_ge(made, nth(5))
            nc.gpsimd.affine_select(out=ident[:, :], in_=ident[:, :], compare_op=ALU.not_equal, fill=1.0,
                                    base=0, pattern=[[-1, P]], channel_multiplier=1).then_inc(made, 1)
            pool.wait_ge(made, nth(6))
            nc.gpsimd.tensor_copy(ident_r[:, :], ident[:, :]).then_inc(made, 1)
            with pool.Fori(0, NI) as rg:
                with pool.Fori(0, BODIES) as bd:
                    turn = rg * BODIES + bd
                    for u in range(UNITS):
                        at, q = turn * UNITS + u, unit(u)[2]
                        if u == 0:
                            pool.wait_ge(deg_clear, nth(rg + 1))
                        pool.wait_ge(adjT_ready, nth(at + 1))
                        part = stored(degp[:, q // 2 * CH:(q // 2 + 1) * CH])[:, :, q % 2 * 2:q % 2 * 2 + 2, :]
                        for slot in range(2):
                            tile = adjT[u % ATB][:, bank(slot)].rearrange("p (a k r) -> p k a r", a=2, k=KT)
                            pool.wait_ge(deg_added, nth(2 * at + slot))
                            nc.gpsimd.tensor_tensor(part, part, tile, ALU.add).then_inc(deg_added, 1)

            def split_y(n, turn):
                pool.wait_ge(y_staged, nth(turn * PAIR + n + 1))
                jc = (turn % BODIES) * PAIR + n
                nc.gpsimd.tensor_tensor(y_lo[n].rearrange("p (w t) -> p w t", w=2),
                                        of_units(y_all[:, bass.ds(jc * CH, CH)], 1),
                                        y_hi[n].bitcast(F32).rearrange("p (w t) -> p w t", w=2),
                                        ALU.subtract).then_inc(y_split, 1)

            def add_beta(g):
                pool.wait_ge(x_res_in, (g + 1) * A * DMA)
                nc.gpsimd.tensor_tensor(by_slot(x_res), by_slot(x_res), vec_all[:, 1:2, :].to_broadcast([P, KT, D]),
                                        ALU.add).then_inc(beta_added, 1)

            def tiles_and_y(turn, mids):
                for u in range(UNITS):
                    _, n, quarter, v = unit(u)
                    if n < mids and u % (UNITS // 2) == MIDS["beta"]:
                        add_beta(2 * turn + 1 + n)
                    if v == 0 and quarter == 0:
                        split_y(n, turn)
                    if v % 2:
                        at = turn * (UNITS // 2) + u // 2
                        pool.wait_ge(hi_ready, nth(at + 1))
                        nc.gpsimd.tensor_tensor(adj_lo[u // 2 % 4], adjT[u % ATB][:, :], adj_hi[u // 2 % 4].bitcast(F32),
                                                ALU.subtract).then_inc(lo_ready, 1)

            pool.wait_ge(vec_done, nth(1))
            add_beta(0)
            with pool.Fori(0, BODIES - 1) as turn:
                tiles_and_y(turn, 2)
            tiles_and_y(BODIES - 1, 1)
            with pool.Fori(BODIES, TURNS) as turn:
                tiles_and_y(turn, 0)

        @block.scalar
        def _(act):
            start("act", act)
            act.wait_ge(const_loaded, 12 * DMA)
            act.wait_ge(made, nth(7))

            def prologue(h):
                for p in range(2):
                    n = 2 * h + p
                    act.wait_ge(mT_ps, nth(n + 1))
                    nc.scalar.activation(mT_sb[p], lg[1][:, :], ACT.Identity, bias=bm_col[:, :]).then_inc(mT_ready, 1)
                    act.wait_ge(scratched, nth(n))
                    act.wait_ge(qk_ps, nth(2 * n + 1))
                    nc.scalar.activation(permuted(q_sb[:, 0, p * CH:(p + 1) * CH]), stored(acc[:, 0:CH]),
                                         ACT.Copy).then_inc(qk_hi, 1)
                    act.wait_ge(qk_ps, nth(2 * n + 2))
                    nc.scalar.activation(k_sb[p][:, 0, :], acc[:, CH:2 * CH], ACT.Copy).then_inc(qk_hi, 1)

            with act.Fori(0, NJ // 2 - 1) as h:
                prologue(h)
            for who in range(2):
                load_chunk(act, who, 0, 0)
            prologue(NJ // 2 - 1)
            for ch in range(1, NAT):
                for who in range(2):
                    load_chunk(act, who, 0, ch)

            with act.Fori(0, NI) as rg:
                with act.Fori(0, BODIES) as bd:
                    turn = rg * BODIES + bd
                    for u in range(UNITS):
                        at = turn * UNITS + u
                        act.wait_ge(gated_ready, nth(at - 1))
                        act.wait_ge(adjT_ready, nth(at + 1))
                        nc.scalar.activation(sq[u % 2], adjT[u % ATB][:, :], ACT.Square).then_inc(sq_ready, 1)
                        act.wait_ge(logits_ready, nth(at + 1))
                        nc.scalar.activation(lg[u % 2][:, :], lg[u % 2][:, :], ACT.Sigmoid, bias=gb_col[:, :],
                                             scale=float(D) ** -0.5).then_inc(probs_ready, 1)
                        if u % V == V - 1:
                            act.wait_ge(adjT_ready, nth(at + 1))
                            next_chunk(act, 1, turn, u // V)
                act.wait_ge(range_done, nth(rg + 1))
                for half in range(HALVES):
                    last = nc.scalar.activation(stored(sT[:, half * CH:(half + 1) * CH]),
                                                permuted(acc[:, half * CH:(half + 1) * CH]), ACT.Copy)
                last.then_inc(acc_read, 1)

            def updated(g):
                if isinstance(g, int):
                    act.wait_ge(agg_kept, nth(NI))
                act.wait_ge(rows_ps, nth(g))
                act.wait_ge(upd_ps, nth(g + 1))
                nc.scalar.activation(u_col, lg[0][:, :], ACT.Relu, bias=bu_col[:, :]).then_inc(upd_ready, 1)

            def deviation(norm, tiles=KT, at=0):
                act.wait_ge(var_ready, nth(norm + 1))
                nc.scalar.activation(sd[:, at:at + tiles], mv[:, at:at + tiles, 1], ACT.Sqrt, bias=eps_col[:, :]).then_inc(sd_ready, 1)

            def make_y(g):
                act.wait_ge(x1_rows, nth(g + 1))
                for k in range(KT):
                    last = nc.scalar.activation(n_rows[:, tile_at(k)], x1_sb[:, tile_at(k)], ACT.Copy,
                                                scale=dinv_now[:, k:k + 1])
                last.then_inc(y_rows, 1)
                act.wait_ge(y_rows, nth(g + 1))
                nc.scalar.activation(y_all[:, bass.ds(g * CH, CH)], n_rows, ACT.Copy)

            def stage_y(n, turn, fresh=False):
                jc = (turn % BODIES) * PAIR + n
                y = n_rows if fresh else y_all[:, bass.ds(jc * CH, CH)]
                nc.scalar.activation(y_sb[n][:, :].rearrange("p (w t) -> p w t", w=2), of_units(y, 0), ACT.Copy)
                nc.scalar.activation(y_hi[n].rearrange("p (w t) -> p w t", w=2), of_units(y, 1),
                                     ACT.Copy).then_inc(y_staged, 1)

            def stage_next(turn, n, fresh=False):
                act.wait_ge(hop_done, nth(turn * UNITS + (0 if n else UNITS // 2)))
                stage_y(n, turn if n else turn + 1, fresh)

            def tile(turn, u):
                if u % 2:
                    act.wait_ge(hop_done, nth(turn * UNITS + u - 7))
                    act.wait_ge(adjT_ready, nth(ALL + turn * UNITS + u + 1))
                    nc.scalar.activation(adj_hi[u // 2 % 4], adjT[u % ATB][:, :], ACT.Copy).then_inc(hi_ready, 1)

            updated(0)
            act.wait_ge(deg_read, nth(NI))
            nc.scalar.activation(root[:, :], deg[:, :], ACT.Sqrt).then_inc(root_ready, 1)
            deviation(0)
            deviation(1)
            updated(1)
            make_y(0)
            stage_y(0, 0, fresh=True)

            def first_range(turn, mids):
                for u in range(UNITS):
                    m, v = u // (UNITS // 2), u % (UNITS // 2)
                    g = 2 * turn + 1 + m
                    tile(turn, u)
                    if u % V == V - 1:
                        next_chunk(act, 1, turn, u // V)
                    if m < mids and v == MIDS["root1"]:
                        deviation(2 * g)
                    if m < mids and v == MIDS["root2"]:
                        deviation(2 * g + 1)
                    if mids == PAIR and v == MIDS["relu"]:
                        updated(g + 1)
                    if v == MIDS["keep"]:
                        if m < mids:
                            make_y(g)
                        stage_next(turn, 1 - m, fresh=m < mids)

            def keep_sums(rg):
                act.wait_ge(hop_range, nth(rg + 1))
                nc.scalar.activation(stored(sT[:, 0:CH]), permuted(acc[:, 0:CH]), ACT.Copy).then_inc(s_half0, 1)

            with act.Fori(0, BODIES - 1) as turn:
                first_range(turn, 2)
            first_range(BODIES - 1, 1)
            keep_sums(0)

            def copy_s(bd, piece):
                act.wait_ge(z_ps, nth(piece))
                nc.scalar.activation(s_piece, sT[:, bass.ds(bd * PIECE, PIECE)], ACT.Copy).then_inc(s_piece_in, 1)

            with act.Fori(1, NI) as rg:
                with act.Fori(0, BODIES) as bd:
                    turn = rg * BODIES + bd
                    piece = turn - BODIES
                    for u in range(UNITS):
                        tile(turn, u)
                        if u % V == V - 1 and u // V + NAT < CHUNKS:
                            next_chunk(act, 1, turn, u // V)
                        elif u % V == V - 1:
                            with act.If(turn < TURNS - 1):
                                next_chunk(act, 1, turn, u // V)
                        if u == LAST["copy"]:
                            act.wait_ge(s_half0, nth(rg))
                            act.wait_ge(s_half1, nth(rg))
                            copy_s(bd, piece)
                        if u == LAST["root"]:
                            deviation(2 * NJ + piece, HT)
                        if u in STAGE:
                            stage_next(turn, 1 - STAGE.index(u))
                keep_sums(rg)
            for n in range(BODIES):
                deviation(2 * NJ + TAIL + n, HT, n % 2 * HT)

        @block.tensor
        def _(pe):
            start("pe", pe)
            def open_sums():
                for b in range(RANGE // BANK):
                    nc.tensor.matmul(acc[:, b * BANK:(b + 1) * BANK], zeros[:, 0:P], zeros[:, :],
                                     start=True, stop=False)

            def close_sums():
                for b in range(RANGE // BANK):
                    last = nc.tensor.matmul(acc[:, b * BANK:(b + 1) * BANK], zeros[:, 0:P], zeros[:, :],
                                            start=False, stop=True)
                return last

            def transposes(dst, src):
                for k in range(KT):
                    last = nc.tensor.transpose(dst[:, k * P:(k + 1) * P], src[:, k * P:(k + 1) * P], ident[:, :])
                return last

            pe.wait_ge(const_loaded, 12 * DMA)
            pe.wait_ge(made, nth(7))
            nc.tensor.matmul(lg[0][:, 0:3 * D], ones_row, vec_rows, start=True, stop=True).then_inc(vec_ps, 1)
            pe.wait_ge(vec_done, nth(1))
            def x_transposed(p, h, n):
                pe.wait_ge(x_in[p], (h + 1) * DMA)
                pe.wait_ge(xT_ready, nth(n))
                transposes(lg[0], x_rows[p]).then_inc(xT_ps, 1)

            x_transposed(0, 0, 0)
            with pe.Fori(0, NJ // 2) as h:
                for p in range(2):
                    n = 2 * h + p
                    pe.wait_ge(xT_ready, nth(n + 1))
                    pe.wait_ge(m_ready, nth(n))
                    for b in range(2):
                        last = nc.tensor.matmul(lg[1][:, bank(b)], w_msg, xT_sb[p][:, bank(b)], start=True, stop=True)
                    last.then_inc(mT_ps, 1)
                    if p == 0:
                        x_transposed(1, h, n + 1)
                    else:
                        with pe.If(h < NJ // 2 - 1):
                            x_transposed(0, h + 1, n + 1)
                    pe.wait_ge(mT_ready, nth(n + 1))
                    transposes(lg[1], mT_sb[p]).then_inc(m_ps, 1)
                    pe.wait_ge(qk_lo, nth(2 * n))
                    for half, w in enumerate((w_q, w_k)):
                        for b in range(2):
                            last = nc.tensor.matmul(acc[:, bank(2 * half + b)], w, mT_sb[p][:, bank(b)],
                                                    start=True, stop=True)
                        last.then_inc(qk_ps, 1)

            def logits(u):
                _, n, quarter, v = unit(u)
                for slot in range(2):
                    for kp, qp in ((0, 0), (0, 1), (1, 0)):
                        last = nc.tensor.matmul(lg[u % 2][:, bank(slot)], k_sb[n][:, kp, tile_at(2 * v + slot)],
                                                q_sb[:, qp, bank(quarter)],
                                                start=(kp == 0 and qp == 0), stop=(kp == 1))
                last.then_inc(logits_ready, 1)

            def aggregate(u):
                _, n, quarter, v = unit(u)
                for slot in range(2):
                    last = nc.tensor.matmul(acc[:, bank(quarter)], m_sb[n][:, tile_at(2 * v + slot)],
                                            gated[u % 2][:, bank(slot)], start=False, stop=False)
                last.then_inc(agg_done, 1)

            def stationary_in(n, turn):
                pe.wait_ge(stat_in[n], turn * 2 * DMA)

            pe.wait_ge(m_ready, nth(NJ))
            pe.wait_ge(qk_lo, nth(2 * NJ))
            logits(0)
            with pe.Fori(0, NI) as rg:
                pe.wait_ge(deg_read, nth(rg))
                open_sums()
                with pe.Fori(0, BODIES) as bd:
                    turn = rg * BODIES + bd
                    for u in range(UNITS):
                        at = turn * UNITS + u
                        if u + 1 < UNITS:
                            _, n, quarter, v = unit(u + 1)
                            if v == 0 and quarter == 2 and n == 0:
                                with pe.If(rg > 0):
                                    pe.wait_ge(q_in[1], rg * DMA)
                            if v == 0 and quarter == 0 and n == 1:
                                with pe.If(turn > 0):
                                    stationary_in(1, turn)
                            pe.wait_ge(gated_ready, nth(at))
                            logits(u + 1)
                        else:
                            with pe.If(turn < TURNS - 1):
                                stationary_in(0, turn + 1)
                                with pe.If(bd > BODIES - 2):
                                    pe.wait_ge(q_in[0], (rg + 1) * DMA)
                                pe.wait_ge(gated_ready, nth(at))
                                logits(0)
                        pe.wait_ge(gated_ready, nth(at + 1))
                        aggregate(u)
                close_sums().then_inc(range_done, 1)
                pe.wait_ge(acc_read, nth(rg + 1))
                pe.wait_ge(deg_added, nth((rg + 1) * BODIES * UNITS * 2))
                for t in range(HALVES * KT):
                    last = nc.tensor.matmul(acc[:, t:t + 1], degp[:, t * P:(t + 1) * P], ones[:, :],
                                            start=True, stop=True)
                last.then_inc(deg_ps, 1)

            def update(g):
                pe.wait_ge(x_col_in, (g + 1) * 2 * DMA)
                pe.wait_ge(upd_ready, nth(g))
                for b in range(2):
                    nc.tensor.matmul(lg[0][:, bank(b)], w_ut[:, :], x_col[:, bank(b)], start=True, stop=False)
                    last = nc.tensor.matmul(lg[0][:, bank(b)], w_ub[:, :], agg_col[:, bank(b)],
                                            start=False, stop=True)
                last.then_inc(upd_ps, 1)

            def rows(g):
                pe.wait_ge(upd_ready, nth(g + 1))
                pe.wait_ge(res_added, nth(g))
                transposes(lg[1], u_col).then_inc(rows_ps, 1)

            for g in range(2):
                update(g)
                rows(g)

            def hop(turn, u):
                _, n, quarter, v = unit(u)
                if v == 0 and quarter == 0:
                    pe.wait_ge(y_staged, nth(turn * PAIR + n + 1))
                if v % 2 == 0:
                    pe.wait_ge(adjT_ready, nth(ALL + turn * UNITS + u + 1))
                    for slot in range(2):
                        last = nc.tensor.matmul(acc[:, bank(quarter)], y_sb[n][:, tile_at(v + slot)],
                                                adjT[u % ATB][:, bank(slot)], start=False, stop=False)
                else:
                    if v == 1 and quarter == 0:
                        pe.wait_ge(y_split, nth(turn * PAIR + n + 1))
                    pe.wait_ge(lo_ready, nth(turn * (UNITS // 2) + u // 2 + 1))
                    hi, lo = adj_hi[u // 2 % 4], adj_lo[u // 2 % 4]
                    for slot in range(2):
                        for y, part in ((y_hi[n], hi), (y_hi[n], lo), (y_lo[n], hi)):
                            last = nc.tensor.matmul(acc[:, bank(quarter)], y[:, tile_at(v - 1 + slot)],
                                                    part[:, bank(slot)], start=False, stop=False)
                last.then_inc(hop_done, 1)

            def first_range(turn, mids):
                for u in range(UNITS):
                    m, v = u // (UNITS // 2), u % (UNITS // 2)
                    g = 2 * turn + 1 + m
                    if mids == PAIR and v == MIDS["upd"]:
                        update(g + 1)
                    if mids == PAIR and v == MIDS["rows"]:
                        rows(g + 1)
                    if u in (2, UNITS // 2 + 2):
                        with pe.If(turn < 1):
                            add_y(u * PAIR // UNITS)
                    hop(turn, u)

            def add_y(n):
                for k in range(KT):
                    at = tile_at(k // 4 * 2 + k % 2)
                    parts = ((y_sb[n], ident),) if k % 4 < 2 else ((y_hi[n], ident_r), (y_lo[n], ident_r))
                    for b in range(2):
                        place = acc[:, bank(2 * n + b)].rearrange("p (a k r) -> p k a r", a=2, k=KT)[:, k]
                        for y, one in parts:
                            nc.tensor.matmul(place, y[:, at], one[:, b * 2 * BLK:(b + 1) * 2 * BLK],
                                             start=False, stop=False)

            pe.wait_ge(deg_read, nth(NI))
            open_sums()
            with pe.Fori(0, BODIES - 1) as turn:
                first_range(turn, 2)
            first_range(BODIES - 1, 1)
            close_sums().then_inc(hop_range, 1)

            def z_product(piece):
                pe.wait_ge(s_piece_in, nth(piece + 1))
                pe.wait_ge(res_used, nth(piece))
                for k in range(HT):
                    last = nc.tensor.matmul(z_bank[0][:, tile_at(k)], s_piece[:, tile_at(k)], w_1[:, :],
                                            start=True, stop=True)
                last.then_inc(z_ps, 1)

            with pe.Fori(1, NI) as rg:
                pe.wait_ge(s_half0, nth(rg))
                pe.wait_ge(s_half1, nth(rg))
                open_sums()
                with pe.Fori(0, BODIES) as bd:
                    turn = rg * BODIES + bd
                    for u in range(UNITS):
                        if u == LAST["z"]:
                            z_product(turn - BODIES)
                        if u in (2, UNITS // 2 + 2):
                            with pe.If(bd == rg):
                                add_y(u * PAIR // UNITS)
                        hop(turn, u)
                close_sums().then_inc(hop_range, 1)
            pe.wait_ge(s_half0, nth(NI))
            pe.wait_ge(s_half1, nth(NI))
            pe.wait_ge(res_used, nth(TAIL))
            for n in range(BODIES):
                for k in range(HT):
                    last = nc.tensor.matmul(z_bank[n][:, tile_at(k)], sT[:, tile_at(n * HT + k)], w_1[:, :],
                                            start=True, stop=True)
                last.then_inc(z_ps, 1)

        @block.vector
        def _(dve):
            start("dve", dve)
            def transpose(u):
                ch, _, _, v = unit(u % UNITS)
                nc.vector.transpose(adjT[u % ATB][:, :].rearrange("p (k c s) -> p k c s", k=2, s=BLK),
                                    nat[ch % NAT][:, :, 2 * v * BLK:(2 * v + 2) * BLK]
                                    .rearrange("p c (k r) -> p k c r", k=2)).then_inc(adjT_ready, 1)

            def wait_chunk(turns, ch):
                for who in range(2):
                    dve.wait_ge(nat_in[ch % NAT][who], (turns * (CHUNKS // NAT) + ch // NAT + 1) * 2 * DMA)

            def next_transpose(turns, u):
                following = u + ATB
                if following % V == 0:
                    wait_chunk(turns + following // UNITS, following % UNITS // V)
                transpose(following)

            dve.wait_ge(vec_ps, nth(1))
            nc.vector.tensor_copy(vec_all[:, :, :].rearrange("p a d -> p (a d)"), lg[0][:, 0:3 * D]).then_inc(vec_done, 1)
            def x_transposed(p, n):
                dve.wait_ge(scratched, nth(n))
                dve.wait_ge(xT_ps, nth(n + 1))
                nc.vector.tensor_copy(stored(xT_sb[p]), permuted(lg[0][:, :])).then_inc(xT_ready, 1)

            x_transposed(0, 0)
            with dve.Fori(0, NJ // 2) as h:
                for p in range(2):
                    n = 2 * h + p
                    dve.wait_ge(m_ps, nth(n + 1))
                    nc.vector.tensor_copy(m_sb[p], lg[1][:, :]).then_inc(m_ready, 1)
                    dve.wait_ge(qk_hi, nth(2 * n + 1))
                    nc.vector.tensor_tensor(permuted(q_sb[:, 1, p * CH:(p + 1) * CH]), stored(acc[:, 0:CH]),
                                            permuted(q_sb[:, 0, p * CH:(p + 1) * CH].bitcast(F32)),
                                            ALU.subtract).then_inc(qk_lo, 1)
                    dve.wait_ge(qk_hi, nth(2 * n + 2))
                    nc.vector.tensor_tensor(k_sb[p][:, 1, :], acc[:, CH:2 * CH], k_sb[p][:, 0, :].bitcast(F32),
                                            ALU.subtract).then_inc(qk_lo, 1)
                    if p == 0:
                        x_transposed(1, n + 1)
                    else:
                        with dve.If(h < NJ // 2 - 1):
                            x_transposed(0, n + 1)

            nc.vector.memset(degp, 0.0).then_inc(deg_clear, 1)
            for u in range(ATB):
                if u % V == 0:
                    wait_chunk(0, u // V)
                if u == 6:
                    dve.wait_ge(scratched, nth(NJ + 1))
                transpose(u)
            with dve.Fori(0, NI) as rg:
                with dve.Fori(0, BODIES) as bd:
                    turn = rg * BODIES + bd
                    for u in range(UNITS):
                        at = turn * UNITS + u
                        dve.wait_ge(agg_done, nth(at - 1))
                        dve.wait_ge(sq_ready, nth(at + 1))
                        dve.wait_ge(probs_ready, nth(at + 1))
                        nc.vector.tensor_tensor(gated[u % 2], lg[u % 2][:, :], sq[u % 2], ALU.mult).then_inc(gated_ready, 1)
                        dve.wait_ge(deg_added, nth(2 * at + 2))
                        next_transpose(turn, u)
                dve.wait_ge(deg_ps, nth(rg + 1))
                nc.vector.tensor_scalar(deg[:, bass.ds(rg * HALVES * KT, HALVES * KT)], acc[:, 0:HALVES * KT],
                                        1.0, None, ALU.add).then_inc(deg_read, 1)
                nc.vector.memset(degp, 0.0).then_inc(deg_clear, 1)

            done = [0]

            def link(last, base):
                done[0] += 1
                last.then_inc(step, 1)
                dve.wait_ge(step, nth(base + done[0]))

            def variances(src, tiles=KT, at=0):
                for k in range(tiles):
                    last = nc.vector.bn_stats(stats[:, at + k, :], src[:, tile_at(k)])
                return last

            def aggregates(tiles=KT, at=0):
                nc.vector.drain()
                for k in range(at, at + tiles):
                    last = nc.vector.bn_aggr(mv[:, k, :], stats[:, k, :])
                last.then_inc(var_ready, 1)

            def normalise(dst, src, base, norm, tiles=KT, at=0):
                dve.wait_ge(var_ready, nth(norm + 1))
                dve.wait_ge(sd_ready, nth(norm + 1))
                link(nc.vector.reciprocal(rstd[:, at:at + tiles], sd[:, at:at + tiles]), base)
                for k in range(tiles):
                    last = nc.vector.tensor_scalar(dst[:, tile_at(k)], src[:, tile_at(k)], mv[:, at + k, 0:1],
                                                   rstd[:, at + k:at + k + 1], ALU.subtract, ALU.mult)
                return last

            def each_row(v, tiles=KT):
                return vec_all[:, v:v + 1, :].to_broadcast([P, tiles, D])

            STEPS = 4
            def rows_stat(g):
                dve.wait_ge(rows_ps, nth(g + 1))
                variances(lg[1])
                aggregates()

            def rows_norm(g):
                done[0] = 0
                base = g * STEPS
                dve.wait_ge(y_staged, nth(g))
                link(normalise(n_rows, lg[1], base, 2 * g), base)
                link(nc.vector.tensor_tensor(by_slot(n_rows), by_slot(n_rows), each_row(0), ALU.mult), base)

            def x1_stat(g):
                dve.wait_ge(beta_added, nth(g + 1))
                nc.vector.tensor_tensor(n_rows, n_rows, x_res, ALU.add).then_inc(res_added, 1)
                dve.wait_ge(res_added, nth(g + 1))
                variances(n_rows)
                aggregates()

            def x1_norm(g):
                base = g * STEPS
                dve.wait_ge(x1_kept, nth(g))
                nc.vector.tensor_copy(dinv_now[:, :], dinv[:, bass.ds(g * KT, KT)])
                normalise(x1_sb, n_rows, base, 2 * g + 1).then_inc(x1_rows, 1)
                assert done[0] == STEPS

            rows_stat(0)
            rows_norm(0)
            x1_stat(0)
            dve.wait_ge(root_ready, nth(1))
            nc.vector.reciprocal(dinv[:, :], root[:, :]).then_inc(dinv_ready, 1)
            dve.wait_ge(dinv_ready, nth(1))
            x1_norm(0)
            rows_stat(1)

            def tile(turn, u):
                if u % 2:
                    dve.wait_ge(lo_ready, nth(turn * (UNITS // 2) + u // 2 + 1))
                else:
                    dve.wait_ge(hop_done, nth(turn * UNITS + u + 1))
                next_transpose(TURNS + turn, u)

            def first_range(turn, mids):
                for u in range(UNITS):
                    m, v = u // (UNITS // 2), u % (UNITS // 2)
                    g = 2 * turn + 1 + m
                    tile(turn, u)
                    if mids == PAIR and v == MIDS["stat1"]:
                        rows_stat(g + 1)
                    if m < mids and v == MIDS["norm1"]:
                        rows_norm(g)
                    if m < mids and v == MIDS["stat2"]:
                        x1_stat(g)
                    if m < mids and v == MIDS["norm2"]:
                        x1_norm(g)

            def keep_sums(rg):
                dve.wait_ge(hop_range, nth(rg + 1))
                dve.wait_ge(s_piece_in, nth(rg * BODIES))
                nc.vector.tensor_copy(stored(sT[:, CH:2 * CH]), permuted(acc[:, CH:2 * CH])).then_inc(s_half1, 1)

            with dve.Fori(0, BODIES - 1) as turn:
                first_range(turn, 2)
            first_range(BODIES - 1, 1)
            keep_sums(0)

            LAST_STEPS = 4
            def piece_stat(piece, base, z_in, loaded, at=0):
                rows = z_rows[at]
                dve.wait_ge(z_ps, nth(piece + 1))
                for k in range(HT):
                    last = nc.vector.tensor_scalar(rows[:, tile_at(k)], z_in[:, tile_at(k)],
                                                   dinv[:, bass.ds(piece * HT + k, 1)], None, ALU.mult)
                link(last, base)
                z = rows.rearrange("p (k d) -> p k d", d=D)
                link(nc.vector.tensor_tensor(z, z, each_row(2, HT), ALU.add), base)
                dve.wait_ge(res_in[at], loaded * DMA)
                link(nc.vector.scalar_tensor_tensor(out=rows, in0=rows, scalar=0.0, in1=res[at],
                                                    op0=ALU.max, op1=ALU.add), base)
                variances(rows, HT, at * HT).then_inc(res_used, 1)
                aggregates(HT, at * HT)

            def piece_norm(piece, base, at=0):
                normalise(results[at], z_rows[at], base, 2 * NJ + piece, HT, at * HT).then_inc(rows_done, 1)

            with dve.Fori(1, NI) as rg:
                with dve.Fori(0, BODIES) as bd:
                    turn = rg * BODIES + bd
                    for u in range(UNITS):
                        if u + ATB < UNITS:
                            tile(turn, u)
                        else:
                            with dve.If(turn < TURNS - 1):
                                tile(turn, u)
                        piece = turn - BODIES
                        base = NJ * STEPS + piece * LAST_STEPS
                        if u == LAST["stat"]:
                            done[0] = 0
                            dve.wait_ge(rows_done, nth(piece))
                            piece_stat(piece, base, z_bank[0], piece + 1)
                        if u == LAST["norm"]:
                            dve.wait_ge(out_free, nth(piece))
                            piece_norm(piece, base)
                            assert done[0] == LAST_STEPS
                keep_sums(rg)

            done[0] = 0
            base = NJ * STEPS + TAIL * LAST_STEPS
            for n in range(BODIES + 1):
                if n < BODIES:
                    dve.wait_ge(rows_done, nth(TAIL + max(0, n - 1)))
                    piece_stat(TAIL + n, base, z_bank[n], (TAIL if n % 2 == 0 else 0) + n // 2 + 1, n % 2)
                if n > 0:
                    dve.wait_ge(out_free, nth(TAIL + max(0, n - 2)))
                    piece_norm(TAIL + n - 1, base, (n - 1) % 2)


_INS = ['x', 'adj', 'L0_gnn_W_msg', 'L0_gnn_b_msg', 'L0_gnn_W_q', 'L0_gnn_W_k', 'L0_gnn_gate_bias',
        'L0_gnn_W_upd', 'L0_gnn_b_upd', 'L0_gnn_ln_gamma', 'L0_gnn_ln_beta', 'L1_gnn_W', 'L1_gnn_b']


def kernel(**inputs):
    import numpy as _np
    import concourse.bacc as _bacc
    from concourse import mybir as _mybir
    from concourse.bass_utils import run_bass_kernel_spmd as _run

    nc = _bacc.Bacc("TRN2", target_bir_lowering=False, num_devices=1)
    arrays, args = {}, []
    for name in _INS:
        a = _np.ascontiguousarray(inputs[name])
        if a.ndim == 0:
            a = a.reshape(1)
        arrays[f"in_{name}"] = a
        args.append(nc.dram_tensor(f"in_{name}", a.shape, _mybir.dt.from_np(a.dtype), kind="ExternalInput").ap())
    args.append(nc.dram_tensor("out_0", (N, D), F32, kind="ExternalOutput").ap())
    build(nc, *args)
    r = _run(nc, [arrays], core_ids=[0])
    return r.results[0]["out_0"]
```

```python
import concourse.bass as bass
from concourse import mybir
from contextlib import ExitStack

F32 = mybir.dt.float32
F32R = mybir.dt.float32r
BF16 = mybir.dt.bfloat16
ALU = mybir.AluOpType
ACT = mybir.ActivationFunctionType

N, D = 8192, 128
P = 128
BLK = 32
CH = 1024
BANK = 512
RANGE = 2048
NJ = N // CH
NI = N // RANGE
A = P // BLK
KT = CH // P
V = KT // 2
C = BANK // BLK
QUARTERS = RANGE // BANK
HALVES = RANGE // CH
PAIR = 2
BODIES = NJ // PAIR
CHUNKS = PAIR * QUARTERS
UNITS = CHUNKS * V
NAT = 4
ATB = 8
HT = KT // 2
PIECE = HT * P
EPS = 1e-5
DMA = 16
START = 8
MIDS = dict(norm1=1, stat2=3, norm2=6, root1=7, root2=11, keep=15,
            upd=8, relu=13, rows=12, stat1=14, beta=12)
STAGE = (5, 21)
DIAGONAL = (0, 1, 6, 7)
TAIL = NI * BODIES - BODIES
CLOSE = 3 * UNITS // 4
OPEN = UNITS // 4
LAST = dict(copy=3, z=2, stat=4, root=10, norm=8)


def build(nc, x, adj, W_msg, b_msg, W_q, W_k, gate_bias, W_upd, b_upd, ln_gamma, ln_beta, W1, b1, out):
    q_dram = nc.dram_tensor("q_split", (P, 2, N), F32, kind="Internal").ap()
    k_dram = nc.dram_tensor("k_split", (P, 2, N), F32, kind="Internal").ap()
    m_dram = nc.dram_tensor("messages", (NJ, P, CH), F32, kind="Internal").ap()
    agg_dram = nc.dram_tensor("aggregated", (P, N), F32, kind="Internal").ap()
    xT_dram = nc.dram_tensor("x_transposed", (P, N), F32, kind="Internal").ap()
    x1_dram = nc.dram_tensor("x_layer1", (2 * NJ, P, PIECE), F32, kind="Internal").ap()

    ctx = ExitStack()
    with ctx:
        def sb(name, shape, dt=F32):
            return ctx.enter_context(nc.sbuf_tensor(name, shape, dt))

        def sem(name):
            return ctx.enter_context(nc.semaphore(name))

        nat = [sb(f"nat{n}", [P, C, CH // A]) for n in range(NAT)]
        adjT = [sb(f"adjT{n}", [P, CH]) for n in range(ATB)]
        q_sb = sb("q_sb", [P, 2, RANGE], F32R)
        k_sb = [sb(f"k_sb{n}", [P, 2, CH], F32R) for n in range(PAIR)]
        split_sb = sb("split_sb", [P, 2, CH], F32R)
        adj_hi = [q_sb[:, 0, n * CH:(n + 1) * CH] for n in range(2)] + [k_sb[n][:, 1, :] for n in range(2)]
        adj_lo = [q_sb[:, 1, n * CH:(n + 1) * CH] for n in range(2)] + [split_sb[:, n, :] for n in range(2)]
        y_hi, y_lo = ([k_sb[n][:, 0, part * PIECE:(part + 1) * PIECE] for n in range(PAIR)] for part in range(2))
        y_sb = [sb(f"y_sb{n}", [P, PIECE]) for n in range(PAIR)]
        work = sb("work", [P, 4, 2 * CH])
        sq = [work[:, 0, n * CH:(n + 1) * CH] for n in range(2)]
        gated = [work[:, 1, n * CH:(n + 1) * CH] for n in range(2)]
        m_sb = [work[:, 2, n * CH:(n + 1) * CH] for n in range(PAIR)]
        degp = work[:, 3, :]
        y_all = work[:, :, :].rearrange("p a b -> p (a b)")
        mT_sb, xT_sb = ([adjT[n + p][:, :] for p in range(2)] for n in (4, 6))
        sT = sb("sT", [P, RANGE])
        agg_col = sb("agg_col", [P, CH])
        x_col = sb("x_col", [P, CH])
        u_col = sT[:, 0:CH]
        stage_a = sb("stage_a", [P, CH])
        stage_b = sb("stage_b", [P, CH])
        stage_c = sb("stage_c", [P, CH])
        x_rows = [stage_a, stage_b]
        x_res, n_rows, x1_sb = stage_a[:, :], stage_b[:, :], stage_c[:, :]
        res_tail = [nat[n][:, 0:2, :].rearrange("p a b -> p (a b)") for n in range(BODIES)]
        res, z_rows, results = ([t[:, n * PIECE:(n + 1) * PIECE] for n in range(2)]
                                for t in (stage_a, stage_b, stage_c))
        s_piece = x_col[:, 0:PIECE]
        ident = sb("ident", [P, P])
        zeros = sb("zeros", [P, BANK], BF16)
        ones = sb("ones", [P, 1])
        w_ut, w_ub, w_1 = (sb(n, [P, D]) for n in ("w_ut", "w_ub", "w_1"))
        w_msg, w_q, w_k = (sT[:, n * D:(n + 1) * D] for n in range(3))
        vec_rows = sT[0:1, CH:CH + 3 * D]
        ones_row = sT[0:1, CH + 3 * D:CH + 3 * D + P]
        bm_col, bu_col, gb_col, eps_col = (sb(n, [P, 1]) for n in ("bm_col", "bu_col", "gb_col", "eps_col"))
        vec_all = sb("vec_all", [P, 3, D])
        deg = sb("deg", [P, NJ * KT])
        root = sb("root", [P, NJ * KT])
        dinv = sb("dinv", [P, NJ * KT])
        dinv_now = sb("dinv_now", [P, KT])
        stats = sb("stats", [P, KT, 6])
        mv = sb("mv", [P, KT, 2])
        sd = sb("sd", [P, KT])
        rstd = sb("rstd", [P, KT])

        acc = ctx.enter_context(nc.psum_tensor("acc", [P, RANGE], F32))
        lg = [ctx.enter_context(nc.psum_tensor(f"lg{n}", [P, CH], F32)) for n in range(2)]

        def sems(*names):
            return [sem(n) for n in names]

        (const_loaded,) = sems("const_loaded")
        kept, kept_x = sems("kept0", "kept1"), sems("kept_x0", "kept_x1")
        x_in = sems("x_in0", "x_in1")
        q_in = sems(*[f"q_in{h}" for h in range(HALVES)])
        stat_in = sems(*[f"stat_in{n}" for n in range(PAIR)])
        nat_in = [sems(f"nat_in{n}_sp", f"nat_in{n}_act") for n in range(NAT)]
        x_col_in, x_res_in, x1_out = sems("x_col_in", "x_res_in", "x1_out")
        (agg_out,) = sems("agg_out")
        res_in, out_done = sems("res_in0", "res_in1"), sems("out_done0", "out_done1")

        started = {}

        def counted_by(engine, *names):
            started.setdefault(engine, []).extend(sems(*names))
            return started[engine][-len(names):]

        def start(engine, eng):
            for s in started[engine]:
                eng.sem_inc(s, START)

        (made,), (vec_ps,), (vec_done,) = (counted_by("pool", "made"), counted_by("pe", "vec_ps"),
                                           counted_by("dve", "vec_done"))
        xT_free, scratched = counted_by("sp", "xT_free", "scratched")
        mT_ready, qk_hi = counted_by("act", "mT_ready", "qk_hi")
        xT_ps, mT_ps, qk_ps, m_ps = counted_by("pe", "xT_ps", "mT_ps", "qk_ps", "m_ps")
        xT_ready, qk_lo, m_ready = counted_by("dve", "xT_ready", "qk_lo", "m_ready")
        adjT_ready, gated_ready = counted_by("dve", "adjT_ready", "gated_ready")
        sq_ready, probs_ready = counted_by("act", "sq_ready", "probs_ready")
        logits_ready, agg_done = counted_by("pe", "logits_ready", "agg_done")
        (deg_added,) = counted_by("pool", "deg_added")
        range_half0, range_half1, deg_ps = counted_by("pe", "range_half0", "range_half1", "deg_ps")
        (acc_half0,), (acc_half1,) = counted_by("act", "acc_half0"), counted_by("dve", "acc_half1")
        (agg_kept,) = counted_by("sp", "agg_kept")
        deg_read, deg_clear = counted_by("dve", "deg_read", "deg_clear")
        root_ready, upd_ready, y_rows = counted_by("act", "root_ready", "upd_ready", "y_rows")
        upd_ps, rows_ps = counted_by("pe", "upd_ps", "rows_ps")
        dinv_ready, res_added, x1_rows = counted_by("dve", "dinv_ready", "res_added", "x1_rows")
        (beta_added,) = counted_by("pool", "beta_added")
        (x1_kept,) = counted_by("sp", "x1_kept")
        var_ready, step = counted_by("dve", "var_ready", "step")
        (sd_ready,) = counted_by("act", "sd_ready")
        y_staged, hi_ready, s_half0, s_piece_in = counted_by("act", "y_staged", "hi_ready", "s_half0", "s_piece_in")
        y_split, lo_ready = counted_by("pool", "y_split", "lo_ready")
        hop_done, hop_half0, hop_half1, z_ps = counted_by("pe", "hop_done", "hop_half0", "hop_half1", "z_ps")
        s_half1, res_used, rows_done = counted_by("dve", "s_half1", "res_used", "rows_done")
        (out_free,) = counted_by("sp", "out_free")

        z_bank = [lg[n // 2][:, n % 2 * PIECE:(n % 2 + 1) * PIECE] for n in range(BODIES)]

        block = ctx.enter_context(nc.Block())

        TURNS = NI * BODIES
        ALL = TURNS * UNITS

        def permuted(t):
            return t.rearrange("p (a k r) -> p k a r", a=A, k=KT)

        def stored(t):
            return t.rearrange("p (k a r) -> p k a r", a=A, k=KT)

        def by_slot(t):
            return t.rearrange("p (k d) -> p k d", k=KT)

        def nth(n):
            return n + START

        def load_chunk(eng, who, turn, ch):
            i0 = (turn // BODIES) * RANGE + (ch % QUARTERS) * BANK
            j0 = (turn % BODIES) * (PAIR * CH) + (ch // QUARTERS) * CH
            for a in (2 * who, 2 * who + 1):
                src = adj[bass.ds(i0, BANK), bass.ds(j0 + a * (CH // A), CH // A)]
                eng.dma_start(nat[ch % NAT][a * BLK:(a + 1) * BLK, :, :],
                              src.rearrange("(c s) w -> s c w", s=BLK)).then_inc(nat_in[ch % NAT][who], DMA)

        def next_chunk(eng, who, turn, ch):
            if ch + NAT < CHUNKS:
                load_chunk(eng, who, turn, ch + NAT)
            else:
                load_chunk(eng, who, (turn + 1) % TURNS, ch + NAT - CHUNKS)

        def unit(u):
            ch = u // V
            return ch, ch // QUARTERS, ch % QUARTERS, u % V

        def bank(b):
            return slice(b * BANK, (b + 1) * BANK)

        def tile_at(k):
            return slice(k * P, (k + 1) * P)

        def of_units(y, split):
            return y.rearrange("p (w s t) -> p w s t", s=2, t=2 * P)[:, :, split, :]

        @block.sync
        def _(sp):
            start("sp", sp)
            sp.sem_inc(xT_free, 1)
            sp.sem_inc(scratched, 1)

            def load_x(p, g):
                sp.dma_start(by_slot(x_rows[p][:, :]),
                             x[bass.ds(g * CH, CH), :].rearrange("(k p) d -> p k d", p=P)).then_inc(x_in[p], DMA)

            def stored_x(p, stores):
                sp.wait_ge(kept_x[p], stores * DMA)
                sp.sem_inc(xT_free, 1)

            def stored_by(p, stores):
                sp.wait_ge(kept[p], stores * DMA)
                sp.sem_inc(scratched, 1)

            def prologue(h, pair, following):
                for p in range(2):
                    n, g = 2 * pair + p, 2 * h + p
                    sp.wait_ge(xT_ready, nth(n + 1))
                    if following is not None:
                        load_x(p, following + p)
                    sp.dma_start(xT_dram[:, bass.ds(g * CH, CH)], xT_sb[p]).then_inc(kept_x[p], DMA)
                    if p == 1:
                        stored_x(0, pair + 1)
                    elif isinstance(pair, int):
                        stored_x(1, pair)
                    else:
                        with sp.If(pair != 0):
                            stored_x(1, pair)
                    sp.wait_ge(qk_lo, nth(2 * n + 2))
                    if following is not None:
                        sp.dma_start(q_dram[:, :, bass.ds(g * CH, CH)], q_sb[:, :, p * CH:(p + 1) * CH].bitcast(F32)
                                     ).then_inc(kept[p], DMA)
                    sp.dma_start(k_dram[:, :, bass.ds(g * CH, CH)], k_sb[p][:, :, :].bitcast(F32)
                                 ).then_inc(kept[p], DMA)
                    sp.wait_ge(m_ready, nth(n + 1))
                    sp.dma_start(m_dram[bass.ds(g, 1), :, :].rearrange("g p w -> (g p) w"), m_sb[p]
                                 ).then_inc(kept[p], DMA)
                    if p == 1:
                        stored_by(0, pair * 3 + (2 if following is None else 3))
                    elif isinstance(pair, int):
                        stored_by(1, pair * 3)
                    else:
                        with sp.If(pair != 0):
                            stored_by(1, pair * 3)

            load_x(0, 2)
            load_x(1, 3)
            for dst, src in ((w_msg, W_msg), (w_q, W_q), (w_k, W_k), (w_1, W1),
                             (w_ut, W_upd[0:D, :]), (w_ub, W_upd[D:2 * D, :])):
                sp.dma_start(dst[:, :], src).then_inc(const_loaded, DMA)
            for dst, src in ((bm_col, b_msg), (bu_col, b_upd)):
                sp.dma_start(dst[:, :], src.rearrange("(d o) -> d o", o=1)).then_inc(const_loaded, DMA)
            sp.dma_start(gb_col[:, :], gate_bias.rearrange("(a b) -> a b", b=1).to_broadcast([P, 1])
                         ).then_inc(const_loaded, DMA)
            for n, src in enumerate((ln_gamma, ln_beta, b1)):
                sp.dma_start(vec_rows[:, n * D:(n + 1) * D], src.rearrange("(a d) -> a d", a=1)
                             ).then_inc(const_loaded, DMA)
            with sp.Fori(1, NJ // 2 - 1) as h:
                prologue(h, h - 1, 2 * h + 2)
            prologue(NJ // 2 - 1, NJ // 2 - 2, 0)
            prologue(0, NJ // 2 - 1, None)
            stored_x(1, NJ // 2)
            stored_by(1, (NJ // 2 - 1) * 3 + 2)

            def load_q(half, rg):
                sp.dma_start(q_sb[:, :, half * CH:(half + 1) * CH].bitcast(F32),
                             q_dram[:, :, bass.ds(rg * RANGE + half * CH, CH)]).then_inc(q_in[half], DMA)

            def load_stationary(n, turn):
                jc = (turn % BODIES) * PAIR + n
                sp.dma_start(k_sb[n][:, :, :].bitcast(F32), k_dram[:, :, bass.ds(jc * CH, CH)]).then_inc(stat_in[n], DMA)
                sp.dma_start(m_sb[n], m_dram[bass.ds(jc, 1), :, :].rearrange("g p w -> (g p) w")
                             ).then_inc(stat_in[n], DMA)

            def load_cols(g):
                sp.wait_ge(upd_ps, nth(g))
                sp.dma_start(x_col[:, :], xT_dram[:, bass.ds(g * CH, CH)]).then_inc(x_col_in, DMA)
                sp.dma_start(agg_col[:, :], agg_dram[:, bass.ds(g * CH, CH)]).then_inc(x_col_in, DMA)

            with sp.Fori(0, NI) as rg:
                with sp.Fori(0, BODIES) as bd:
                    turn = rg * BODIES + bd
                    for ch in range(CHUNKS):
                        if ch == CHUNKS - 2:
                            with sp.If(bd > BODIES - 2):
                                with sp.If(rg < NI - 1):
                                    sp.wait_ge(logits_ready, nth(turn * UNITS + ch * V))
                                    load_q(0, (rg + 1) % NI)
                        sp.wait_ge(adjT_ready, nth(turn * UNITS + (ch + 1) * V))
                        next_chunk(sp, 0, turn, ch)
                        if ch % QUARTERS == QUARTERS - 1:
                            with sp.If(turn < TURNS - 1):
                                sp.wait_ge(agg_done, nth(turn * UNITS + (ch + 1) * V))
                                load_stationary(ch // QUARTERS, (turn + 1) % TURNS)
                with sp.If(rg < NI - 1):
                    sp.wait_ge(logits_ready, nth((rg + 1) * BODIES * UNITS))
                    load_q(1, (rg + 1) % NI)
                with sp.If(rg > NI - 2):
                    load_cols(0)
                sp.wait_ge(acc_half0, nth(rg + 1))
                sp.wait_ge(acc_half1, nth(rg + 1))
                sp.dma_start(agg_dram[:, bass.ds(rg * RANGE, RANGE)], sT[:, :]).then_inc(agg_out, DMA)
                sp.wait_ge(agg_out, (rg + 1) * DMA)
                sp.sem_inc(agg_kept, 1)

            def load_x_res(g):
                sp.wait_ge(res_added, nth(g))
                for a in range(A):
                    src = x[bass.ds(g * CH + a * (CH // A), CH // A), :].rearrange("(k r) d -> r k d", r=BLK)
                    sp.dma_start(by_slot(stage_a[a * BLK:(a + 1) * BLK, :]), src).then_inc(x_res_in, DMA)

            def store_x1(g):
                sp.wait_ge(x1_rows, nth(g + 1))
                sp.dma_start(x1_dram[bass.ds(2 * g, 2), :, :].rearrange("h p w -> p h w"),
                             x1_sb.rearrange("p (h w) -> p h w", h=2)).then_inc(x1_out, DMA)

            def x1_stored(g):
                sp.wait_ge(x1_out, (g + 1) * DMA)
                sp.sem_inc(x1_kept, 1)

            def chunk(turn, ch):
                sp.wait_ge(adjT_ready, nth(ALL + turn * UNITS + (ch + 1) * V))
                next_chunk(sp, 0, turn, ch)

            load_x_res(0)
            load_cols(1)
            load_x_res(1)
            store_x1(0)
            x1_stored(0)
            with sp.Fori(0, BODIES - 1) as bd:
                for ch in range(CHUNKS):
                    g = 2 * bd + 1 + ch // QUARTERS
                    if ch % QUARTERS == 1:
                        load_cols(g + 1)
                    if ch % QUARTERS == 2:
                        load_x_res(g + 1)
                    chunk(bd, ch)
                    if ch % QUARTERS == QUARTERS - 1:
                        store_x1(g)
                        x1_stored(g)
            for ch in range(CHUNKS):
                chunk(BODIES - 1, ch)
                if ch == QUARTERS - 1:
                    store_x1(NJ - 1)
                    x1_stored(NJ - 1)

            def load_res(piece, at=0):
                sp.dma_start(res[at], x1_dram[bass.ds(piece, 1), :, :].rearrange("h p w -> (h p) w")
                             ).then_inc(res_in[at], DMA)

            def store_results(piece, at=0):
                sp.wait_ge(rows_done, nth(piece + 1))
                for a in range(A):
                    row = (piece // 2) * CH + (piece % 2) * (HT * BLK) + a * (CH // A)
                    dst = out[bass.ds(row, HT * BLK), :].rearrange("(k r) d -> r k d", r=BLK)
                    sp.dma_start(dst, results[at][a * BLK:(a + 1) * BLK, :].rearrange("p (k d) -> p k d", k=HT)
                                 ).then_inc(out_done[at], DMA)

            sp.wait_ge(res_added, nth(NJ))
            load_res(0)
            with sp.Fori(1, NI) as rg:
                with sp.Fori(0, BODIES) as bd:
                    turn = rg * BODIES + bd
                    piece = turn - BODIES
                    for ch in range(CHUNKS):
                        if ch == 3:
                            store_results(piece)
                            load_res(piece + 1)
                        if ch + NAT < CHUNKS:
                            chunk(turn, ch)
                        else:
                            with sp.If(turn < TURNS - 1):
                                chunk(turn, ch)
                        if ch == CHUNKS - 1:
                            sp.wait_ge(out_done[0], (piece + 1) * A * DMA)
                            sp.sem_inc(out_free, 1)
            sp.wait_ge(adjT_ready, nth(2 * ALL))
            for n in range(1, BODIES):
                sp.dma_start(res_tail[n], x1_dram[TAIL + n]).then_inc(res_in[1], DMA)
            for n in range(BODIES):
                store_results(TAIL + n, n % 2)
                if n + 2 < BODIES:
                    sp.wait_ge(out_done[n % 2], ((TAIL if n % 2 == 0 else 0) + n // 2 + 1) * A * DMA)
                    sp.sem_inc(out_free, 1)
            sp.wait_ge(out_done[0], (TAIL + 2) * A * DMA)
            sp.wait_ge(out_done[1], 2 * A * DMA)

        @block.gpsimd
        def _(pool):
            start("pool", pool)
            nc.gpsimd.memset(ident[:, :], 0.0).then_inc(made, 1)
            nc.gpsimd.memset(zeros[:, :], 0.0).then_inc(made, 1)
            nc.gpsimd.memset(ones[:, :], 1.0).then_inc(made, 1)
            nc.gpsimd.memset(ones_row, 1.0).then_inc(made, 1)
            nc.gpsimd.memset(eps_col[:, :], EPS).then_inc(made, 1)
            pool.wait_ge(made, nth(5))
            nc.gpsimd.affine_select(out=ident[:, :], in_=ident[:, :], compare_op=ALU.not_equal, fill=1.0,
                                    base=0, pattern=[[-1, P]], channel_multiplier=1).then_inc(made, 1)
            with pool.Fori(0, NI) as rg:
                with pool.Fori(0, BODIES) as bd:
                    turn = rg * BODIES + bd
                    for u in range(UNITS):
                        at, q = turn * UNITS + u, unit(u)[2]
                        if u in (0, 2 * V):
                            pool.wait_ge(deg_clear, nth(2 * rg + 1 + u // (2 * V)))
                        pool.wait_ge(adjT_ready, nth(at + 1))
                        part = stored(degp[:, q // 2 * CH:(q // 2 + 1) * CH])[:, :, q % 2 * 2:q % 2 * 2 + 2, :]
                        for slot in range(2):
                            tile = adjT[u % ATB][:, bank(slot)].rearrange("p (a k r) -> p k a r", a=2, k=KT)
                            pool.wait_ge(deg_added, nth(2 * at + slot))
                            nc.gpsimd.tensor_tensor(part, part, tile, ALU.add).then_inc(deg_added, 1)

            def split_y(n, turn):
                pool.wait_ge(y_staged, nth(turn * PAIR + n + 1))
                jc = (turn % BODIES) * PAIR + n
                nc.gpsimd.tensor_tensor(y_lo[n].rearrange("p (w t) -> p w t", w=2),
                                        of_units(y_all[:, bass.ds(jc * CH, CH)], 1),
                                        y_hi[n].bitcast(F32).rearrange("p (w t) -> p w t", w=2),
                                        ALU.subtract).then_inc(y_split, 1)

            def add_beta(g):
                pool.wait_ge(x_res_in, (g + 1) * A * DMA)
                nc.gpsimd.tensor_tensor(by_slot(x_res), by_slot(x_res), vec_all[:, 1:2, :].to_broadcast([P, KT, D]),
                                        ALU.add).then_inc(beta_added, 1)

            def tiles_and_y(turn, mids):
                for u in range(UNITS):
                    _, n, quarter, v = unit(u)
                    if mids == PAIR and u % (UNITS // 2) == MIDS["beta"]:
                        add_beta(2 * turn + 2 + n)
                    if v == 0 and quarter == 0:
                        split_y(n, turn)
                    if v % 2:
                        at = turn * (UNITS // 2) + u // 2
                        pool.wait_ge(hi_ready, nth(at + 1))
                        nc.gpsimd.tensor_tensor(adj_lo[u // 2 % 4], adjT[u % ATB][:, :], adj_hi[u // 2 % 4].bitcast(F32),
                                                ALU.subtract).then_inc(lo_ready, 1)

            pool.wait_ge(vec_done, nth(1))
            add_beta(0)
            add_beta(1)
            with pool.Fori(0, BODIES - 1) as turn:
                tiles_and_y(turn, 2)
            tiles_and_y(BODIES - 1, 1)
            with pool.Fori(BODIES, TURNS) as turn:
                tiles_and_y(turn, 0)

        @block.scalar
        def _(act):
            start("act", act)
            act.wait_ge(const_loaded, 12 * DMA)
            act.wait_ge(made, nth(6))

            def prologue(h):
                for p in range(2):
                    n = 2 * h + p
                    act.wait_ge(mT_ps, nth(n + 1))
                    nc.scalar.activation(mT_sb[p], lg[1][:, :], ACT.Identity, bias=bm_col[:, :]).then_inc(mT_ready, 1)
                    act.wait_ge(scratched, nth(n))
                    act.wait_ge(qk_ps, nth(2 * n + 1))
                    nc.scalar.activation(permuted(q_sb[:, 0, p * CH:(p + 1) * CH]), stored(acc[:, 0:CH]),
                                         ACT.Copy).then_inc(qk_hi, 1)
                    act.wait_ge(qk_ps, nth(2 * n + 2))
                    nc.scalar.activation(k_sb[p][:, 0, :], acc[:, CH:2 * CH], ACT.Copy).then_inc(qk_hi, 1)

            with act.Fori(0, NJ // 2 - 1) as h:
                prologue(h)
            for ch in range(NAT):
                if ch == NAT // 2:
                    prologue(NJ // 2 - 1)
                for who in range(2):
                    load_chunk(act, who, 0, ch)

            def square(at, u):
                act.wait_ge(gated_ready, nth(at - 1))
                act.wait_ge(adjT_ready, nth(at + 1))
                nc.scalar.activation(sq[u % 2], adjT[u % ATB][:, :], ACT.Square).then_inc(sq_ready, 1)

            square(0, 0)
            with act.Fori(0, NI) as rg:
                with act.Fori(0, BODIES) as bd:
                    turn = rg * BODIES + bd
                    for u in range(UNITS):
                        at = turn * UNITS + u
                        act.wait_ge(logits_ready, nth(at + 1))
                        nc.scalar.activation(lg[u % 2][:, :], lg[u % 2][:, :], ACT.Sigmoid, bias=gb_col[:, :],
                                             scale=float(D) ** -0.5).then_inc(probs_ready, 1)
                        if u + 1 < UNITS:
                            square(at + 1, u + 1)
                        else:
                            with act.If(turn < TURNS - 1):
                                square(at + 1, 0)
                        if u == CLOSE + 2:
                            with act.If(bd > BODIES - 2):
                                act.wait_ge(agg_kept, nth(rg))
                                act.wait_ge(range_half0, nth(rg + 1))
                                nc.scalar.activation(stored(sT[:, 0:CH]), permuted(acc[:, 0:CH]),
                                                     ACT.Copy).then_inc(acc_half0, 1)
                        if u % V == V - 1:
                            act.wait_ge(adjT_ready, nth(at + 1))
                            next_chunk(act, 1, turn, u // V)

            def updated(g):
                if isinstance(g, int):
                    act.wait_ge(agg_kept, nth(NI))
                act.wait_ge(rows_ps, nth(g))
                act.wait_ge(upd_ps, nth(g + 1))
                nc.scalar.activation(u_col, lg[0][:, :], ACT.Relu, bias=bu_col[:, :]).then_inc(upd_ready, 1)

            def deviation(norm, tiles=KT, at=0):
                act.wait_ge(var_ready, nth(norm + 1))
                nc.scalar.activation(sd[:, at:at + tiles], mv[:, at:at + tiles, 1], ACT.Sqrt, bias=eps_col[:, :]).then_inc(sd_ready, 1)

            def make_y(g):
                act.wait_ge(x1_rows, nth(g + 1))
                for k in range(KT):
                    last = nc.scalar.activation(n_rows[:, tile_at(k)], x1_sb[:, tile_at(k)], ACT.Copy,
                                                scale=dinv_now[:, k:k + 1])
                last.then_inc(y_rows, 1)
                act.wait_ge(y_rows, nth(g + 1))
                nc.scalar.activation(y_all[:, bass.ds(g * CH, CH)], n_rows, ACT.Copy)

            def stage_y(n, turn, fresh=False):
                jc = (turn % BODIES) * PAIR + n
                y = n_rows if fresh else y_all[:, bass.ds(jc * CH, CH)]
                nc.scalar.activation(y_sb[n][:, :].rearrange("p (w t) -> p w t", w=2), of_units(y, 0), ACT.Copy)
                nc.scalar.activation(y_hi[n].rearrange("p (w t) -> p w t", w=2), of_units(y, 1),
                                     ACT.Copy).then_inc(y_staged, 1)

            def stage_next(turn, n, fresh=False):
                act.wait_ge(hop_done, nth(turn * UNITS + (0 if n else UNITS // 2)))
                stage_y(n, turn if n else turn + 1, fresh)

            def tile(turn, u):
                if u % 2:
                    act.wait_ge(hop_done, nth(turn * UNITS + u - 7))
                    act.wait_ge(adjT_ready, nth(ALL + turn * UNITS + u + 1))
                    nc.scalar.activation(adj_hi[u // 2 % 4], adjT[u % ATB][:, :], ACT.Copy).then_inc(hi_ready, 1)

            updated(0)
            act.wait_ge(deg_read, nth(NI))
            nc.scalar.activation(root[:, :], deg[:, :], ACT.Sqrt).then_inc(root_ready, 1)
            deviation(0)
            deviation(1)
            updated(1)
            make_y(0)
            stage_y(0, 0, fresh=True)

            def first_range(turn, mids):
                for u in range(UNITS):
                    m, v = u // (UNITS // 2), u % (UNITS // 2)
                    g = 2 * turn + 1 + m
                    tile(turn, u)
                    if u % V == V - 1:
                        next_chunk(act, 1, turn, u // V)
                    if m < mids and v == MIDS["root1"]:
                        deviation(2 * g)
                    if m < mids and v == MIDS["root2"]:
                        deviation(2 * g + 1)
                    if mids == PAIR and v == MIDS["relu"]:
                        updated(g + 1)
                    if v == MIDS["keep"]:
                        if m < mids:
                            make_y(g)
                        stage_next(turn, 1 - m, fresh=m < mids)

            def keep_sums(rg):
                act.wait_ge(hop_half0, nth(rg + 1))
                nc.scalar.activation(stored(sT[:, 0:CH]), permuted(acc[:, 0:CH]), ACT.Copy).then_inc(s_half0, 1)

            with act.Fori(0, BODIES - 1) as turn:
                first_range(turn, 2)
            first_range(BODIES - 1, 1)
            keep_sums(0)

            def copy_s(bd, piece):
                act.wait_ge(z_ps, nth(piece))
                nc.scalar.activation(s_piece, sT[:, bass.ds(bd * PIECE, PIECE)], ACT.Copy).then_inc(s_piece_in, 1)

            with act.Fori(1, NI) as rg:
                with act.Fori(0, BODIES) as bd:
                    turn = rg * BODIES + bd
                    piece = turn - BODIES
                    for u in range(UNITS):
                        tile(turn, u)
                        if u % V == V - 1 and u // V + NAT < CHUNKS:
                            next_chunk(act, 1, turn, u // V)
                        elif u % V == V - 1:
                            with act.If(turn < TURNS - 1):
                                next_chunk(act, 1, turn, u // V)
                        if u == LAST["copy"]:
                            act.wait_ge(s_half0, nth(rg))
                            act.wait_ge(s_half1, nth(rg))
                            copy_s(bd, piece)
                        if u == LAST["root"]:
                            deviation(2 * NJ + piece, HT)
                        if u in STAGE:
                            stage_next(turn, 1 - STAGE.index(u))
                keep_sums(rg)
            for n in range(BODIES):
                deviation(2 * NJ + TAIL + n, HT, n % 2 * HT)

        @block.tensor
        def _(pe):
            start("pe", pe)
            def open_sums(half):
                for b in (2 * half, 2 * half + 1):
                    nc.tensor.matmul(acc[:, bank(b)], zeros[:, 0:P], zeros[:, :], start=True, stop=False)

            def close_sums(half):
                for b in (2 * half, 2 * half + 1):
                    last = nc.tensor.matmul(acc[:, bank(b)], zeros[:, 0:P], zeros[:, :], start=False, stop=True)
                return last

            def transposes(dst, src):
                for k in range(KT):
                    last = nc.tensor.transpose(dst[:, k * P:(k + 1) * P], src[:, k * P:(k + 1) * P], ident[:, :])
                return last

            pe.wait_ge(const_loaded, 12 * DMA)
            pe.wait_ge(made, nth(6))
            nc.tensor.matmul(lg[0][:, 0:3 * D], ones_row, vec_rows, start=True, stop=True).then_inc(vec_ps, 1)
            pe.wait_ge(vec_done, nth(1))
            def x_transposed(p, h, n):
                pe.wait_ge(x_in[p], (h + 1) * DMA)
                pe.wait_ge(xT_ready, nth(n))
                transposes(lg[0], x_rows[p]).then_inc(xT_ps, 1)

            x_transposed(0, 0, 0)
            with pe.Fori(0, NJ // 2) as h:
                for p in range(2):
                    n = 2 * h + p
                    pe.wait_ge(xT_ready, nth(n + 1))
                    pe.wait_ge(m_ready, nth(n))
                    for b in range(2):
                        last = nc.tensor.matmul(lg[1][:, bank(b)], w_msg, xT_sb[p][:, bank(b)], start=True, stop=True)
                    last.then_inc(mT_ps, 1)
                    if p == 0:
                        x_transposed(1, h, n + 1)
                    else:
                        with pe.If(h < NJ // 2 - 1):
                            x_transposed(0, h + 1, n + 1)
                    pe.wait_ge(mT_ready, nth(n + 1))
                    transposes(lg[1], mT_sb[p]).then_inc(m_ps, 1)
                    pe.wait_ge(qk_lo, nth(2 * n))
                    for half, w in enumerate((w_q, w_k)):
                        for b in range(2):
                            last = nc.tensor.matmul(acc[:, bank(2 * half + b)], w, mT_sb[p][:, bank(b)],
                                                    start=True, stop=True)
                        last.then_inc(qk_ps, 1)

            def logits(u):
                _, n, quarter, v = unit(u)
                for slot in range(2):
                    for kp, qp in ((0, 0), (0, 1), (1, 0)):
                        last = nc.tensor.matmul(lg[u % 2][:, bank(slot)], k_sb[n][:, kp, tile_at(2 * v + slot)],
                                                q_sb[:, qp, bank(quarter)],
                                                start=(kp == 0 and qp == 0), stop=(kp == 1))
                last.then_inc(logits_ready, 1)

            def aggregate(u):
                _, n, quarter, v = unit(u)
                for slot in range(2):
                    last = nc.tensor.matmul(acc[:, bank(quarter)], m_sb[n][:, tile_at(2 * v + slot)],
                                            gated[u % 2][:, bank(slot)], start=False, stop=False)
                last.then_inc(agg_done, 1)

            def stationary_in(n, turn):
                pe.wait_ge(stat_in[n], turn * 2 * DMA)

            pe.wait_ge(m_ready, nth(NJ))
            pe.wait_ge(qk_lo, nth(2 * NJ))
            logits(0)
            with pe.Fori(0, NI) as rg:
                pe.wait_ge(acc_half0, nth(rg))
                open_sums(0)
                with pe.Fori(0, BODIES) as bd:
                    turn = rg * BODIES + bd
                    for u in range(UNITS):
                        at = turn * UNITS + u
                        if u + 1 < UNITS:
                            _, n, quarter, v = unit(u + 1)
                            if v == 0 and quarter == 2 and n == 0:
                                with pe.If(rg > 0):
                                    pe.wait_ge(q_in[1], rg * DMA)
                            if v == 0 and quarter == 0 and n == 1:
                                with pe.If(turn > 0):
                                    stationary_in(1, turn)
                            pe.wait_ge(gated_ready, nth(at))
                            if u == 0:
                                pe.wait_ge(deg_read, nth(rg))
                            logits(u + 1)
                        else:
                            with pe.If(turn < TURNS - 1):
                                stationary_in(0, turn + 1)
                                with pe.If(bd > BODIES - 2):
                                    pe.wait_ge(q_in[0], (rg + 1) * DMA)
                                pe.wait_ge(gated_ready, nth(at))
                                logits(0)
                        if u == OPEN:
                            with pe.If(bd < 1):
                                pe.wait_ge(acc_half1, nth(rg))
                                open_sums(1)
                        pe.wait_ge(gated_ready, nth(at + 1))
                        aggregate(u)
                        if u == CLOSE - 1:
                            with pe.If(bd > BODIES - 2):
                                close_sums(0).then_inc(range_half0, 1)
                close_sums(1).then_inc(range_half1, 1)
                pe.wait_ge(deg_added, nth((rg + 1) * BODIES * UNITS * 2))
                for t in range(HALVES * KT):
                    last = nc.tensor.matmul(lg[1][:, t:t + 1], degp[:, t * P:(t + 1) * P], ones[:, :],
                                            start=True, stop=True)
                last.then_inc(deg_ps, 1)

            def update(g):
                pe.wait_ge(x_col_in, (g + 1) * 2 * DMA)
                pe.wait_ge(upd_ready, nth(g))
                for b in range(2):
                    nc.tensor.matmul(lg[0][:, bank(b)], w_ut[:, :], x_col[:, bank(b)], start=True, stop=False)
                    last = nc.tensor.matmul(lg[0][:, bank(b)], w_ub[:, :], agg_col[:, bank(b)],
                                            start=False, stop=True)
                last.then_inc(upd_ps, 1)

            def rows(g):
                pe.wait_ge(upd_ready, nth(g + 1))
                pe.wait_ge(res_added, nth(g))
                if isinstance(g, int):
                    pe.wait_ge(deg_read, nth(NI))
                transposes(lg[1], u_col).then_inc(rows_ps, 1)

            for g in range(2):
                update(g)
                rows(g)

            def hop(turn, u):
                _, n, quarter, v = unit(u)
                if v == 0 and quarter == 0:
                    pe.wait_ge(y_staged, nth(turn * PAIR + n + 1))
                if v % 2 == 0:
                    pe.wait_ge(adjT_ready, nth(ALL + turn * UNITS + u + 1))
                    for slot in range(2):
                        last = nc.tensor.matmul(acc[:, bank(quarter)], y_sb[n][:, tile_at(v + slot)],
                                                adjT[u % ATB][:, bank(slot)], start=False, stop=False)
                else:
                    if v == 1 and quarter == 0:
                        pe.wait_ge(y_split, nth(turn * PAIR + n + 1))
                    pe.wait_ge(lo_ready, nth(turn * (UNITS // 2) + u // 2 + 1))
                    hi, lo = adj_hi[u // 2 % 4], adj_lo[u // 2 % 4]
                    for slot in range(2):
                        for y, part in ((y_hi[n], hi), (y_hi[n], lo), (y_lo[n], hi)):
                            last = nc.tensor.matmul(acc[:, bank(quarter)], y[:, tile_at(v - 1 + slot)],
                                                    part[:, bank(slot)], start=False, stop=False)
                last.then_inc(hop_done, 1)

            def first_range(turn, mids):
                for u in range(UNITS):
                    m, v = u // (UNITS // 2), u % (UNITS // 2)
                    g = 2 * turn + 1 + m
                    if mids == PAIR and v == MIDS["upd"]:
                        update(g + 1)
                    if mids == PAIR and v == MIDS["rows"]:
                        rows(g + 1)
                    hop(turn, u)
                    if mids < PAIR and u == CLOSE - 1:
                        close_sums(0).then_inc(hop_half0, 1)

            open_sums(0)
            open_sums(1)
            with pe.Fori(0, BODIES - 1) as turn:
                first_range(turn, 2)
            first_range(BODIES - 1, 1)
            close_sums(1).then_inc(hop_half1, 1)

            def z_product(piece):
                pe.wait_ge(s_piece_in, nth(piece + 1))
                pe.wait_ge(res_used, nth(piece))
                for k in range(HT):
                    last = nc.tensor.matmul(z_bank[0][:, tile_at(k)], s_piece[:, tile_at(k)], w_1[:, :],
                                            start=True, stop=True)
                last.then_inc(z_ps, 1)

            with pe.Fori(1, NI) as rg:
                pe.wait_ge(s_half0, nth(rg))
                open_sums(0)
                with pe.Fori(0, BODIES) as bd:
                    turn = rg * BODIES + bd
                    for u in range(UNITS):
                        if u == LAST["z"]:
                            z_product(turn - BODIES)
                        if u == OPEN:
                            with pe.If(bd < 1):
                                pe.wait_ge(s_half1, nth(rg))
                                open_sums(1)
                        hop(turn, u)
                        if u == CLOSE - 1:
                            with pe.If(bd > BODIES - 2):
                                close_sums(0).then_inc(hop_half0, 1)
                close_sums(1).then_inc(hop_half1, 1)
            pe.wait_ge(s_half0, nth(NI))
            pe.wait_ge(s_half1, nth(NI))
            pe.wait_ge(res_used, nth(TAIL))
            for n in range(BODIES):
                for k in range(HT):
                    last = nc.tensor.matmul(z_bank[n][:, tile_at(k)], sT[:, tile_at(n * HT + k)], w_1[:, :],
                                            start=True, stop=True)
                last.then_inc(z_ps, 1)

        @block.vector
        def _(dve):
            start("dve", dve)
            def transpose(u):
                ch, _, _, v = unit(u % UNITS)
                nc.vector.transpose(adjT[u % ATB][:, :].rearrange("p (k c s) -> p k c s", k=2, s=BLK),
                                    nat[ch % NAT][:, :, 2 * v * BLK:(2 * v + 2) * BLK]
                                    .rearrange("p c (k r) -> p k c r", k=2)).then_inc(adjT_ready, 1)

            def wait_chunk(turns, ch):
                for who in range(2):
                    dve.wait_ge(nat_in[ch % NAT][who], (turns * (CHUNKS // NAT) + ch // NAT + 1) * 2 * DMA)

            def add_identity(turns, u, own):
                ch = (u + ATB) % UNITS // V
                if u % V or ch not in DIAGONAL:
                    return
                with dve.If(own):
                    wait_chunk(turns + (u + ATB) // UNITS, ch)
                    identity_onto(ch)

            def identity_onto(ch):
                for a in range(2):
                    group = slice((ch % 2 * 2 + a) * BLK, (ch % 2 * 2 + a + 1) * BLK)
                    rows = nat[ch % NAT][group, :, :].rearrange("p c w -> p (c w)")
                    stride = CH // A + BLK
                    place = rows[:, a * (C * CH // A - KT * stride):][:, 0:KT * stride].rearrange(
                        "p (k w) -> p k w", w=stride)[:, :, a * (CH // A):a * (CH // A) + BLK]
                    one = ident[group, group].rearrange("p (o r) -> p o r", o=1).to_broadcast([BLK, KT, BLK])
                    nc.vector.tensor_tensor(place, place, one, ALU.add)
                nc.vector.drain()

            def next_transpose(turns, u):
                following = u + ATB
                if following % V == 0:
                    wait_chunk(turns + following // UNITS, following % UNITS // V)
                transpose(following)

            dve.wait_ge(vec_ps, nth(1))
            nc.vector.tensor_copy(vec_all[:, :, :].rearrange("p a d -> p (a d)"), lg[0][:, 0:3 * D]).then_inc(vec_done, 1)
            def x_transposed(p, n):
                dve.wait_ge(xT_free, nth(n))
                dve.wait_ge(xT_ps, nth(n + 1))
                nc.vector.tensor_copy(stored(xT_sb[p]), permuted(lg[0][:, :])).then_inc(xT_ready, 1)

            x_transposed(0, 0)
            with dve.Fori(0, NJ // 2) as h:
                for p in range(2):
                    n = 2 * h + p
                    dve.wait_ge(scratched, nth(n))
                    dve.wait_ge(m_ps, nth(n + 1))
                    nc.vector.tensor_copy(m_sb[p], lg[1][:, :]).then_inc(m_ready, 1)
                    if p == 0:
                        x_transposed(1, n + 1)
                    else:
                        with dve.If(h < NJ // 2 - 1):
                            x_transposed(0, n + 1)
                    dve.wait_ge(qk_hi, nth(2 * n + 1))
                    nc.vector.tensor_tensor(permuted(q_sb[:, 1, p * CH:(p + 1) * CH]), stored(acc[:, 0:CH]),
                                            permuted(q_sb[:, 0, p * CH:(p + 1) * CH].bitcast(F32)),
                                            ALU.subtract).then_inc(qk_lo, 1)
                    dve.wait_ge(qk_hi, nth(2 * n + 2))
                    nc.vector.tensor_tensor(k_sb[p][:, 1, :], acc[:, CH:2 * CH], k_sb[p][:, 0, :].bitcast(F32),
                                            ALU.subtract).then_inc(qk_lo, 1)

            for u in range(ATB):
                if u % V == 0:
                    wait_chunk(0, u // V)
                if u == 6:
                    dve.wait_ge(xT_free, nth(NJ + 1))
                transpose(u)
            def read_deg(rg):
                dve.wait_ge(deg_ps, nth(rg))
                nc.vector.tensor_scalar(deg[:, bass.ds((rg + NI - 1) % NI * (HALVES * KT), HALVES * KT)], lg[1][:, 0:HALVES * KT],
                                        1.0, None, ALU.add).then_inc(deg_read, 1)

            def keep_half1(rg):
                dve.wait_ge(agg_kept, nth(rg - 1))
                dve.wait_ge(range_half1, nth(rg))
                nc.vector.tensor_copy(stored(sT[:, CH:2 * CH]), permuted(acc[:, CH:2 * CH])).then_inc(acc_half1, 1)

            with dve.Fori(0, NI) as rg:
                with dve.Fori(0, BODIES) as bd:
                    turn = rg * BODIES + bd
                    for u in range(UNITS):
                        at = turn * UNITS + u
                        dve.wait_ge(agg_done, nth(at - 1))
                        dve.wait_ge(sq_ready, nth(at + 1))
                        dve.wait_ge(probs_ready, nth(at + 1))
                        nc.vector.tensor_tensor(gated[u % 2], lg[u % 2][:, :], sq[u % 2], ALU.mult).then_inc(gated_ready, 1)
                        if u in (0, 2):
                            with dve.If(bd < 1):
                                with dve.If(rg > 0):
                                    (keep_half1 if u else read_deg)(rg)
                                nc.vector.memset(degp[:, u // 2 * CH:(u // 2 + 1) * CH], 0.0).then_inc(deg_clear, 1)
                        if u + ATB >= UNITS:
                            add_identity(turn, u, turn > TURNS - 2)
                        dve.wait_ge(deg_added, nth(2 * at + 2))
                        next_transpose(turn, u)
            read_deg(NI)
            keep_half1(NI)

            done = [0]

            def link(last, base):
                done[0] += 1
                last.then_inc(step, 1)
                dve.wait_ge(step, nth(base + done[0]))

            def variances(src, tiles=KT, at=0):
                for k in range(tiles):
                    last = nc.vector.bn_stats(stats[:, at + k, :], src[:, tile_at(k)])
                return last

            def aggregates(tiles=KT, at=0):
                nc.vector.drain()
                for k in range(at, at + tiles):
                    last = nc.vector.bn_aggr(mv[:, k, :], stats[:, k, :])
                last.then_inc(var_ready, 1)

            def normalise(dst, src, base, norm, tiles=KT, at=0):
                dve.wait_ge(var_ready, nth(norm + 1))
                dve.wait_ge(sd_ready, nth(norm + 1))
                link(nc.vector.reciprocal(rstd[:, at:at + tiles], sd[:, at:at + tiles]), base)
                for k in range(tiles):
                    last = nc.vector.tensor_scalar(dst[:, tile_at(k)], src[:, tile_at(k)], mv[:, at + k, 0:1],
                                                   rstd[:, at + k:at + k + 1], ALU.subtract, ALU.mult)
                return last

            def each_row(v, tiles=KT):
                return vec_all[:, v:v + 1, :].to_broadcast([P, tiles, D])

            STEPS = 4
            def rows_stat(g):
                dve.wait_ge(rows_ps, nth(g + 1))
                variances(lg[1])
                aggregates()

            def rows_norm(g):
                done[0] = 0
                base = g * STEPS
                dve.wait_ge(y_staged, nth(g))
                link(normalise(n_rows, lg[1], base, 2 * g), base)
                link(nc.vector.tensor_tensor(by_slot(n_rows), by_slot(n_rows), each_row(0), ALU.mult), base)

            def x1_stat(g):
                dve.wait_ge(beta_added, nth(g + 1))
                nc.vector.tensor_tensor(n_rows, n_rows, x_res, ALU.add).then_inc(res_added, 1)
                dve.wait_ge(res_added, nth(g + 1))
                variances(n_rows)
                aggregates()

            def x1_norm(g):
                base = g * STEPS
                dve.wait_ge(x1_kept, nth(g))
                nc.vector.tensor_copy(dinv_now[:, :], dinv[:, bass.ds(g * KT, KT)])
                normalise(x1_sb, n_rows, base, 2 * g + 1).then_inc(x1_rows, 1)
                assert done[0] == STEPS

            rows_stat(0)
            rows_norm(0)
            x1_stat(0)
            dve.wait_ge(root_ready, nth(1))
            nc.vector.reciprocal(dinv[:, :], root[:, :]).then_inc(dinv_ready, 1)
            dve.wait_ge(dinv_ready, nth(1))
            x1_norm(0)
            rows_stat(1)

            def tile(turn, u, own=None):
                if own is not None:
                    add_identity(TURNS + turn, u, own)
                if u % 2:
                    dve.wait_ge(lo_ready, nth(turn * (UNITS // 2) + u // 2 + 1))
                else:
                    dve.wait_ge(hop_done, nth(turn * UNITS + u + 1))
                next_transpose(TURNS + turn, u)

            def first_range(turn, mids):
                for u in range(UNITS):
                    m, v = u // (UNITS // 2), u % (UNITS // 2)
                    g = 2 * turn + 1 + m
                    tile(turn, u, turn < 1 if mids == PAIR and u + ATB < UNITS else None)
                    if mids == PAIR and v == MIDS["stat1"]:
                        rows_stat(g + 1)
                    if m < mids and v == MIDS["norm1"]:
                        rows_norm(g)
                    if m < mids and v == MIDS["stat2"]:
                        x1_stat(g)
                    if m < mids and v == MIDS["norm2"]:
                        x1_norm(g)

            def keep_sums(rg):
                dve.wait_ge(hop_half1, nth(rg + 1))
                dve.wait_ge(s_piece_in, nth(rg * BODIES))
                nc.vector.tensor_copy(stored(sT[:, CH:2 * CH]), permuted(acc[:, CH:2 * CH])).then_inc(s_half1, 1)

            with dve.Fori(0, BODIES - 1) as turn:
                first_range(turn, 2)
            first_range(BODIES - 1, 1)
            keep_sums(0)

            LAST_STEPS = 4
            def piece_stat(piece, base, n, at=0):
                rows = z_rows[at]
                dve.wait_ge(z_ps, nth(piece + 1))
                for k in range(HT):
                    last = nc.vector.tensor_scalar(rows[:, tile_at(k)], z_bank[n][:, tile_at(k)],
                                                   dinv[:, bass.ds(piece * HT + k, 1)], None, ALU.mult)
                link(last, base)
                z = rows.rearrange("p (k d) -> p k d", d=D)
                link(nc.vector.tensor_tensor(z, z, each_row(2, HT), ALU.add), base)
                residual = res_tail[n] if n else res[0]
                if n == 0:
                    dve.wait_ge(res_in[0], (piece + 1) * DMA)
                else:
                    dve.wait_ge(res_in[1], (BODIES - 1) * DMA)
                link(nc.vector.scalar_tensor_tensor(out=rows, in0=rows, scalar=0.0, in1=residual,
                                                    op0=ALU.max, op1=ALU.add), base)
                variances(rows, HT, at * HT).then_inc(res_used, 1)
                aggregates(HT, at * HT)

            def piece_norm(piece, base, at=0):
                normalise(results[at], z_rows[at], base, 2 * NJ + piece, HT, at * HT).then_inc(rows_done, 1)

            with dve.Fori(1, NI) as rg:
                with dve.Fori(0, BODIES) as bd:
                    turn = rg * BODIES + bd
                    for u in range(UNITS):
                        if u + ATB < UNITS:
                            tile(turn, u, bd == rg)
                        else:
                            with dve.If(turn < TURNS - 1):
                                tile(turn, u, bd == rg - 1)
                        piece = turn - BODIES
                        base = NJ * STEPS + piece * LAST_STEPS
                        if u == LAST["stat"]:
                            done[0] = 0
                            dve.wait_ge(rows_done, nth(piece))
                            piece_stat(piece, base, 0)
                        if u == LAST["norm"]:
                            dve.wait_ge(out_free, nth(piece))
                            piece_norm(piece, base)
                            assert done[0] == LAST_STEPS
                keep_sums(rg)

            done[0] = 0
            base = NJ * STEPS + TAIL * LAST_STEPS
            for n in range(BODIES + 1):
                if n < BODIES:
                    dve.wait_ge(rows_done, nth(TAIL + max(0, n - 1)))
                    piece_stat(TAIL + n, base, n, n % 2)
                if n > 0:
                    dve.wait_ge(out_free, nth(TAIL + max(0, n - 2)))
                    piece_norm(TAIL + n - 1, base, (n - 1) % 2)


_INS = ['x', 'adj', 'L0_gnn_W_msg', 'L0_gnn_b_msg', 'L0_gnn_W_q', 'L0_gnn_W_k', 'L0_gnn_gate_bias',
        'L0_gnn_W_upd', 'L0_gnn_b_upd', 'L0_gnn_ln_gamma', 'L0_gnn_ln_beta', 'L1_gnn_W', 'L1_gnn_b']


def kernel(**inputs):
    import numpy as _np
    import concourse.bacc as _bacc
    from concourse import mybir as _mybir
    from concourse.bass_utils import run_bass_kernel_spmd as _run

    nc = _bacc.Bacc("TRN2", target_bir_lowering=False, num_devices=1)
    arrays, args = {}, []
    for name in _INS:
        a = _np.ascontiguousarray(inputs[name])
        if a.ndim == 0:
            a = a.reshape(1)
        arrays[f"in_{name}"] = a
        args.append(nc.dram_tensor(f"in_{name}", a.shape, _mybir.dt.from_np(a.dtype), kind="ExternalInput").ap())
    args.append(nc.dram_tensor("out_0", (N, D), F32, kind="ExternalOutput").ap())
    build(nc, *args)
    r = _run(nc, [arrays], core_ids=[0])
    return r.results[0]["out_0"]
```
